# Optimizing a Trainium2 kernel written in Bass

```python
import numpy as np
import jax
import jax.numpy as jnp

def _softmax(x, axis=-1):
    return jax.nn.softmax(x, axis=axis)

def _gelu(x):
    return jax.nn.gelu(x, approximate=True)

def _silu(x):
    return jax.nn.silu(x)

def _sigmoid(x):
    return jax.nn.sigmoid(x)

def _layernorm(x, axis=-1, eps=1e-05):
    m = jnp.mean(x, axis=axis, keepdims=True)
    v = jnp.var(x, axis=axis, keepdims=True)
    return (x - m) / jnp.sqrt(v + eps)

def _scatter_add(tgt, idx, src, axis=0):
    return tgt.at[idx].add(src)

def _segment_sum(src, seg, n):
    return jax.ops.segment_sum(src, seg, n)
kernel_name = 'mk_cond_seq_d2_seqx_r4_20015c'

def setup_inputs(seed: int=0):
    np.random.seed(seed)
    _w = jnp.asarray

    def _rec_inputs():
        import jax
        import jax.numpy as jnp
        _rk = jax.random.key(seed)
        x = -0.0003482 + 1 * jax.random.normal(jax.random.fold_in(_rk, 1), (8, 512, 288), jnp.float32)
        _lenS = 512 - jax.random.randint(jax.random.fold_in(_rk, 7), (8,), 0, max(1, 512 // 4) + 1, jnp.int32)
        _lenS2 = 512 - jax.random.randint(jax.random.fold_in(_rk, 8), (8,), 0, max(1, 512 // 4) + 1, jnp.int32)
        cond_1152 = 0.00257642 + 1.0011 * jax.random.normal(jax.random.fold_in(_rk, 11), (8, 288), jnp.float32)
        return (x, cond_1152)
    x, cond_1152 = _rec_inputs()

    def _L0_cond_setup():
        import jax, jax.numpy as jnp
        import numpy as np
        from jax.scipy.linalg import expm
        N, D, COND_DIM = (288, 64, 288)
        B, T = (16, 256)

        def _rotation(cond, W, b):
            v = jax.nn.silu(cond) @ W.T + b
            iu, ju = jnp.triu_indices(D, k=1)
            A = jnp.zeros((cond.shape[0], D, D), dtype=v.dtype)
            A = A.at[:, iu, ju].set(v).at[:, ju, iu].set(-v)
            return expm(A)
        key = jax.random.key(seed)
        k1, k2, k3, k4, k5 = jax.random.split(key, 5)
        x = jax.random.normal(k1, (B, T, N), dtype=jnp.float32)
        cond = jax.random.normal(k2, (B, COND_DIM), dtype=jnp.float32)
        P = jax.random.normal(k3, (N, D), dtype=jnp.float32)
        n_skew = D * (D - 1) // 2
        bound = 1.0 / np.sqrt(COND_DIM)
        W = jax.random.uniform(k4, (n_skew, COND_DIM), minval=-bound, maxval=bound, dtype=jnp.float32)
        b = jax.random.uniform(k5, (n_skew,), minval=-bound, maxval=bound, dtype=jnp.float32)
        return {'x': x, 'cond': cond, 'P': P, 'W': W, 'b': b}
    _L0_cond_all = _L0_cond_setup()
    _L0_cond_in = {k: v for k, v in _L0_cond_all.items() if k in ('P', 'W', 'b')}
    del _L0_cond_all

    def _L1_cond_setup():
        import jax, jax.numpy as jnp
        import numpy as np
        NUM_HEADS = 16
        NUM_EXPERTS = 4
        TOP_K = 2
        LN_EPS = 1e-06

        def _ln(h):
            mu = jnp.mean(h, axis=-1, keepdims=True)
            var = jnp.var(h, axis=-1, keepdims=True)
            return (h - mu) * jax.lax.rsqrt(var + LN_EPS)

        def _modulate(h, shift, scale):
            return h * (1.0 + scale[:, None, :]) + shift[:, None, :]
        key = jax.random.key(seed)
        ks = jax.random.split(key, 12)
        B, N, C = (8, 256, 288)
        H = 4 * C
        E = NUM_EXPERTS
        s = 0.02
        return {'x': jax.random.normal(ks[0], (B, N, C), jnp.float32), 'c': jax.random.normal(ks[1], (B, C), jnp.float32), 'w_adaln': jax.random.normal(ks[2], (C, 6 * C), jnp.float32) * s, 'b_adaln': jnp.zeros((6 * C,), jnp.float32), 'w_qkv': jax.random.normal(ks[3], (C, 3 * C), jnp.float32) * s, 'b_qkv': jnp.zeros((3 * C,), jnp.float32), 'w_proj': jax.random.normal(ks[4], (C, C), jnp.float32) * s, 'b_proj': jnp.zeros((C,), jnp.float32), 'w_gate': jax.random.normal(ks[5], (C, E), jnp.float32) * s, 'w1': jax.random.normal(ks[6], (E, C, H), jnp.float32) * s, 'b1': jnp.zeros((E, H), jnp.float32), 'w2': jax.random.normal(ks[7], (E, H, C), jnp.float32) * s, 'b2': jnp.zeros((E, C), jnp.float32)}
    _L1_cond_all = _L1_cond_setup()
    _L1_cond_in = {k: v for k, v in _L1_cond_all.items() if k in ('w_adaln', 'b_adaln', 'w_qkv', 'b_qkv', 'w_proj', 'b_proj', 'w_gate', 'w1', 'b1', 'w2', 'b2')}
    del _L1_cond_all
    return {'x': x, 'cond_1152': cond_1152, 'L0_cond_P': _L0_cond_in['P'], 'L0_cond_W': _L0_cond_in['W'], 'L0_cond_b': _L0_cond_in['b'], 'L1_cond_w_adaln': _L1_cond_in['w_adaln'], 'L1_cond_b_adaln': _L1_cond_in['b_adaln'], 'L1_cond_w_qkv': _L1_cond_in['w_qkv'], 'L1_cond_b_qkv': _L1_cond_in['b_qkv'], 'L1_cond_w_proj': _L1_cond_in['w_proj'], 'L1_cond_b_proj': _L1_cond_in['b_proj'], 'L1_cond_w_gate': _L1_cond_in['w_gate'], 'L1_cond_w1': _L1_cond_in['w1'], 'L1_cond_b1': _L1_cond_in['b1'], 'L1_cond_w2': _L1_cond_in['w2'], 'L1_cond_b2': _L1_cond_in['b2']}

def reference(x, cond_1152, L0_cond_P, L0_cond_W, L0_cond_b, L1_cond_w_adaln, L1_cond_b_adaln, L1_cond_w_qkv, L1_cond_b_qkv, L1_cond_w_proj, L1_cond_b_proj, L1_cond_w_gate, L1_cond_w1, L1_cond_b1, L1_cond_w2, L1_cond_b2):
    import jax
    import jax.numpy as jnp

    def _L0_cond_ref(x, cond, P, W, b):
        import jax, jax.numpy as jnp
        import numpy as np
        from jax.scipy.linalg import expm
        N, D, COND_DIM = (288, 64, 288)
        B, T = (16, 256)

        def _rotation(cond, W, b):
            v = jax.nn.silu(cond) @ W.T + b
            iu, ju = jnp.triu_indices(D, k=1)
            A = jnp.zeros((cond.shape[0], D, D), dtype=v.dtype)
            A = A.at[:, iu, ju].set(v).at[:, ju, iu].set(-v)
            return expm(A)
        U, _ = jnp.linalg.qr(P)
        R = _rotation(cond, W, b)
        z = jnp.einsum('btn,nd->btd', x, U)
        z_rot = jnp.einsum('btd,bde->bte', z, R)
        x_rot = x + jnp.einsum('btd,nd->btn', z_rot - z, U)
        return x_rot

    def _L1_cond_ref(x, c, w_adaln, b_adaln, w_qkv, b_qkv, w_proj, b_proj, w_gate, w1, b1, w2, b2):
        import jax, jax.numpy as jnp
        import numpy as np
        NUM_HEADS = 16
        NUM_EXPERTS = 4
        TOP_K = 2
        LN_EPS = 1e-06

        def _ln(h):
            mu = jnp.mean(h, axis=-1, keepdims=True)
            var = jnp.var(h, axis=-1, keepdims=True)
            return (h - mu) * jax.lax.rsqrt(var + LN_EPS)

        def _modulate(h, shift, scale):
            return h * (1.0 + scale[:, None, :]) + shift[:, None, :]
        B, N, C = x.shape
        nh = NUM_HEADS
        hd = C // nh
        mod = jax.nn.silu(c) @ w_adaln + b_adaln
        sh_msa, sc_msa, g_msa, sh_mlp, sc_mlp, g_mlp = jnp.split(mod, 6, axis=-1)
        h = _modulate(_ln(x), sh_msa, sc_msa)
        qkv = (h @ w_qkv + b_qkv).reshape(B, N, 3, nh, hd).transpose(2, 0, 3, 1, 4)
        q, k, v = (qkv[0], qkv[1], qkv[2])
        attn = jax.nn.softmax(jnp.einsum('bhqd,bhkd->bhqk', q, k) * hd ** (-0.5), axis=-1)
        o = jnp.einsum('bhqk,bhkd->bhqd', attn, v).transpose(0, 2, 1, 3).reshape(B, N, C)
        o = o @ w_proj + b_proj
        x = x + g_msa[:, None, :] * o
        xn = _modulate(_ln(x), sh_mlp, sc_mlp)
        xf = xn.reshape(-1, C)
        gate_logits = xf @ w_gate
        topk_logits, topk_idx = jax.lax.top_k(gate_logits, TOP_K)
        gates = jax.nn.softmax(topk_logits, axis=-1)
        cw = jnp.sum(jax.nn.one_hot(topk_idx, NUM_EXPERTS, dtype=xf.dtype) * gates[..., None], axis=1)
        hmid = jax.nn.gelu(jnp.einsum('tc,ech->eth', xf, w1) + b1[:, None, :], approximate=True)
        eo = jnp.einsum('eth,ehc->etc', hmid, w2) + b2[:, None, :]
        moe = jnp.einsum('te,etc->tc', cw, eo).reshape(B, N, C)
        return x + g_mlp[:, None, :] * moe
    x = _L0_cond_ref(x, cond_1152, L0_cond_P, L0_cond_W, L0_cond_b)
    x = _L1_cond_ref(x, cond_1152, L1_cond_w_adaln, L1_cond_b_adaln, L1_cond_w_qkv, L1_cond_b_qkv, L1_cond_w_proj, L1_cond_b_proj, L1_cond_w_gate, L1_cond_w1, L1_cond_b1, L1_cond_w2, L1_cond_b2)
    return x

_drawn_inputs = setup_inputs


def setup_inputs(seed=0):
    import zlib

    import numpy as np

    out = dict(_drawn_inputs(seed))
    spreads = {'L1_cond_b_adaln': (0.0, 0.441),
     'L1_cond_b_qkv': (0.0, 0.8),
     'L1_cond_b_proj': (0.0, 0.381),
     'L1_cond_b1': (0.0, 0.8),
     'L1_cond_b2': (0.0, 0.53)}
    factors = {'L1_cond_w_qkv': 8.0,
     'L1_cond_w_proj': 5.937,
     'L1_cond_w_gate': 3.001,
     'L1_cond_w1': 2.827}
    for name, (base, spread) in spreads.items():
        noise = np.random.default_rng([zlib.crc32(name.encode()), seed]).standard_normal(out[name].shape)
        drawn = base * np.exp(spread * noise) if base else spread * noise
        out[name] = jnp.asarray(drawn.astype(out[name].dtype))
    for name, factor in factors.items():
        out[name] = (out[name] * factor).astype(out[name].dtype)
    return out
```

```python
from contextlib import ExitStack

import concourse.bass as bass
from concourse import mybir

F32 = mybir.dt.float32
F32R = mybir.dt.float32r
BF16 = mybir.dt.bfloat16
ALU = mybir.AluOpType
ACT = mybir.ActivationFunctionType
AX = mybir.AxisListType

NB, T, C = 8, 512, 288
NT = T // 128
D = 64
CH = 96
NCH = C // CH
NH = 16
HD = C // NH
HP = 7
MT = 5
MROWS = [HP * HD] * 4 + [2 * C - 4 * HP * HD]
NPAIR = 6
KROWS = NPAIR * HD
NPART = 3
SCALE = HD ** -0.5
NE = 4
HID = 1152
HT = HID // 128
STACK = 96
XW = 256 + STACK
VW = 20
NSQ = 16
NG = NE * NB

PS_UPT, PS_RST, PS_FS, PS_A2, PS_A3, PS_A4, PS_H1, PS_H2, PS_RT, PS_S, PS_VT, PS_XT = range(1, 13)
FLAGS_SPREAD, A2_DONE, A3_DONE, A4_DONE, RT_DONE, VT_DONE = range(1, 7)
SKEW_DONE, ROWSUM_DONE, FLAGS_DONE, SCALED_DONE, B2_DONE, H1_DONE, R_DONE, X_DONE = range(1, 9)
UP_DONE, DIAG_DONE, OMF_DONE = range(1, 4)

TAYLOR = [1.0]
for _k in range(1, 12):
    TAYLOR.append(TAYLOR[-1] / _k)


def build(nc, x, condT, P, WT, bU, w_adaln, b_adaln, w_qkv, b_qkv, w_proj, b_proj, w_gate, w1, b1T, w2, b2, out):
    up_d = nc.dram_tensor("up_scratch", (NB, D, D), F32).ap()
    gate_d = nc.dram_tensor("gate_scratch", (NB, 2, C), F32).ap()
    rot_d = nc.dram_tensor("rot_scratch", (NB, D, C), F32).ap()
    mod_d = nc.dram_tensor("mod_scratch", (NB, 128, 12), F32).ap()
    qk_d = nc.dram_tensor("qk_scratch", (2 * NH, NPART, HD, T), BF16).ap()
    xn_d = nc.dram_tensor("xn_scratch", (NB, 128, 5, T), F32).ap()

    with ExitStack() as ctx:
        def sb(name, shape, dt=F32, c=ctx):
            return c.enter_context(nc.sbuf_tensor(name, shape, dt))

        def sem(name):
            return ctx.enter_context(nc.semaphore(name))

        R = [ctx.enter_context(nc.psum_tensor(f"ringR{k}", [128, 512], F32)) for k in range(2)]
        ST = [ctx.enter_context(nc.psum_tensor(f"ringS{k}", [128, 2, 512], F32)) for k in range(2)]
        OB = [ctx.enter_context(nc.psum_tensor(f"bankO{k}", [128, 512], F32)) for k in range(2)]
        bank = [R[0][:], R[1][:], ST[0][:, 0], ST[0][:, 1], ST[1][:, 0], ST[1][:, 1], OB[0][:], OB[1][:]]

        ident = sb("ident", [128, 128])
        identb = sb("identb", [128, 128], BF16)
        ones = sb("ones", [128, 128])
        nhalf = sb("nhalf", [128, 4])
        X2 = sb("X2", [128, NB, NT, C])
        cw = sb("cw", [128, NB, NT, NE])

        ab = ctx.enter_context(ExitStack())
        wqh = sb("wqh", [128, 3, 3 * C], F32R, ab)
        wql = sb("wql", [128, 2, 3 * C], F32R, ab)
        wp = sb("wp", [CH, NCH, C], F32, ab)
        wgh = sb("wgh", [128, 3, NE], F32R, ab)
        wgl = sb("wgl", [128, 2, NE], F32R, ab)
        b2s = sb("b2s", [NE, C], F32, ab)
        bqk = sb("bqk", [128, MT], F32, ab)
        bv = sb("bv", [128, C], F32, ab)
        bp = sb("bp", [128, C], F32, ab)
        U = sb("U", [CH, NCH, D], F32, ab)

        a = ctx.enter_context(ExitStack())
        wqr = sb("wqr", [128, 3, 3 * C], F32, a)
        wgr = sb("wgr", [128, 3, NE], F32, a)
        A = sb("A", [CH, NCH, D], F32, a)
        V0 = sb("V0", [CH, D], F32, a)
        a0m = sb("a0m", [CH, 2], F32, a)
        maskge = sb("maskge", [CH, D], F32, a)
        striu = sb("striu", [D, D], F32, a)
        Es = sb("Es", [CH, D], F32, a)
        sc = sb("sc", [CH, 16], F32, a)
        t1 = sb("t1", [CH, D], F32, a)
        cc = sb("cc", [CH, D], F32, a)
        VT = sb("VT", [D, C], F32, a)
        XX = sb("XX", [D, 2, D], F32, a)
        Y = sb("Y", [D, D], F32, a)
        UT = sb("UT", [D, C], F32, a)
        dd = sb("dd", [D, 4], F32, a)
        sT = sb("sT", [CH, NCH, NB], F32, a)
        cT = sb("cT", [CH, NCH, NB], F32, a)
        eT = sb("eT", [CH, NCH, NB], F32, a)
        wad = sb("wad", [CH, NCH, 6 * C], F32, a)
        wad2 = sb("wad2", [CH, NCH, 4, STACK], F32, a)
        bad = sb("bad", [1, 6 * C], F32, a)
        bad2 = sb("bad2", [1, 4, STACK], F32, a)
        modt = sb("modt", [128, NB, 12], F32, a)
        gts = sb("gts", [1, 2, 2, C], F32, a)
        wts = sb("wts", [CH, 4, NCH, 512], F32, a)
        vf = sb("vf", [NB, D * D], F32, a)
        bUs = sb("bUs", [D, D], F32, a)
        Ab = sb("Ab", [D, NB, D], F32, a)
        A2 = sb("A2", [D, NB, D], F32, a)
        A3 = sb("A3", [D, NB, D], F32, a)
        A4 = sb("A4", [D, NB, D], F32, a)
        Bk = sb("Bk", [D, NB, D], F32, a)
        RR = sb("RR", [D, NB, D], F32, a)
        RT = sb("RT", [D, NB, D], F32, a)
        L = sb("L", [D, NB, D], F32, a)
        LT = sb("LT", [D, NB, D], F32, a)
        gI = sb("gI", [D, NB, D], F32, a)
        rs = sb("rs", [D, NB], F32, a)
        nrm = sb("nrm", [NB, 2], F32, a)
        pw = sb("pw", [NB, 2, NSQ], F32, a)
        fs = sb("fs", [NB, NSQ + 1], F32, a)
        fq = sb("fq", [NB, NSQ], F32, a)
        dg = sb("dg", [NB, NB, NSQ + 1], F32, a)
        fsb = sb("fsb", [D, NB, NSQ + 1], F32, a)
        omf = sb("omf", [D, NB, NSQ], F32, a)
        Gs = sb("Gs", [D, NB, C], F32, a)
        a.close()

        Qs = sb("Qs", [128, NH, T], BF16, ab)
        Ks = sb("Ks", [128, NH, T], BF16, ab)
        PT = sb("PT", [128, 2, NT, T], F32, ab)
        Va = sb("Va", [128, NT, NH, VW], F32, ab)
        xin = sb("xin", [128, NT, C], F32, ab)
        xT = sb("xT", [CH, NCH, T], F32, ab)
        zT = sb("zT", [D, T], F32, ab)
        oTh = sb("oTh", [VW, T], F32, ab)
        st6 = sb("st6", [128, 2, NT, 6], F32, ab)
        mv = sb("mv", [128, 2, NT, 2], F32, ab)
        ve = sb("ve", [128, 2, NT], F32, ab)
        rstd = sb("rstd", [128, 2, NT], F32, ab)
        xh = sb("xh", [128, NT, XW], F32, ab)
        F = sb("F", [128, 3, T], F32, ab)
        Hh = sb("Hh", [128, 3, T], F32R, ab)
        Hl = sb("Hl", [128, 2, T], F32R, ab)
        Nh = sb("Nh", [128, 3, T], F32R, ab)
        Nl = sb("Nl", [128, 2, T], F32R, ab)
        QF = sb("QF", [128, 2, T], F32, ab)
        prt = sb("prt", [128, 2, NPART, T], BF16, ab)
        mx = sb("mx", [128, NT, NH // NT, NT], F32, ab)
        mr = sb("mr", [128, 16], F32, ab)
        mp = sb("mp", [128, NPART, 16], BF16, ab)
        mTs = sb("mTs", [48, 2, 128], BF16, ab)
        rec = sb("rec", [128, 2, NT, 2], F32, ab)
        o = sb("o", [128, NT, C], F32, ab)
        gat = sb("gat", [128, 2, C], F32, ab)
        rot = sb("rot", [D, C], F32, ab)
        modf = sb("modf", [128, 12], F32, ab)
        modn = sb("modn", [128, 12], F32, ab)
        yt = sb("yt", [128, 2, C], F32, ab)
        lg = sb("lg", [128, NT, NE], F32, ab)
        k1 = sb("k1", [128, NT, NE], F32, ab)
        k2 = sb("k2", [128, NT, NE], F32, ab)
        us = sb("us", [128, NT, NE], F32, ab)
        l2 = sb("l2", [128, NT, NE], F32, ab)
        m12 = sb("m12", [128, 4, NT], F32, ab)
        ab.close()

        wr = sb("wr", [128, HT, 3, 128], F32)
        vr = sb("vr", [128, HT, C], F32)
        w1h = sb("w1h", [128, HT, 3, 128], F32R)
        w1l = sb("w1l", [128, HT, 2, 128], F32R)
        w2h = sb("w2h", [128, HT, C], F32R)
        w2l = sb("w2l", [128, HT, C], F32R)
        b1s = sb("b1s", [128, NE * HT])
        xn = sb("xn", [128, 2, 5, T], F32R)
        gc = sb("gc", [128, 2, C])
        GF = sb("GF", [128, 3, T])
        Gh = sb("Gh", [128, 3, T], F32R)
        Gl = sb("Gl", [128, 3, T], F32R)
        et = sb("et", [128, 4, C])

        names = """const ld_P ld_cond ld_wad ld_misc ld_wq ld_bU
 e_silu s_silu p_mods mods p_gates gates mod_out p_vf vf_ready vf_out up_in expm_pool expm_ps expm_dve expm_act 
 
 lr_ready p_sq sq_ready rotm p_rot rot_ready rot_out
 qrE qrD sigma upd a0 V_ready XT_ready p_Y Y_ready p_X p_U U_ready 
 wq_split dch pch
 kones vones ld_x ld_rot ld_modf ld_modn ld_gat
 xT_ps xT_sb z_ps z_sb delta_ps xrot bst mvf var_eps rstd_f xh_f1 hT_ps hF hHi hLo
 qk_ps qkF qkh qkr qkm qkl v_ps v_sb s_ps smax mparts mT_ps mT_sb st_ps expd av_ps avT tok_ps orec o_sb oT_ps oT_sb proj_ps yg x2_1
 bst2 mvn var_eps2 rstd_n xh_n nT_ps nF nHi nLo xn_out
 gl_ps lgc top g_exp cw_ready cwT_ps cwT_sb b2_ps b2g x2_2
 ld_b1 w_free w_hi w_lo m1_ps gelu ghi glo m2_ps eg acc apart""".split()
        S = {n: sem(n) for n in names}
        qin = [sem(f"qk_in_quad{k}") for k in range(4)]
        wraw = [sem(f"w_raw{t}") for t in range(HT)]
        ld_wt = [sem(f"ld_wt{k}") for k in range(4)]
        gate_out = [sem(f"gate_out{k}") for k in range(2)]
        parts_out = [sem(f"parts_out{k}") for k in range(2)]
        m_in = [sem(f"max_in{k}") for k in range(2)]
        ld_xn = [sem(f"ld_xn{k}") for k in range(2)]
        ld_gc = [sem(f"ld_gc{k}") for k in range(2)]
        yout = sem("y_stored")

        block = ctx.enter_context(nc.Block())

        def fixed(i, n):
            return isinstance(i, int) and i == n

        def parts_stored(i, m):
            return (i * (3 - m % 2) + (m // 2 + 1)) * NPART * 16

        tok = OB[1][:, 0:NT * 2 * VW].rearrange("p (t s d) -> p t s d", t=NT, s=2)

        def m1_bank(t):
            return (ST[0][:, 0, :], ST[0][:, 1, :], ST[1][:, 0, :])[t % 3]

        def m2_bank(t):
            return (R[0][:], R[1][:], OB[0][:], OB[1][:])[t]

        def wait_apart(engine, sem, value):
            engine.wait_ge(sem, value)
            engine.sem_inc(S["apart"], 1)

        def bc(ap, shape):
            return ap.to_broadcast(shape)

        @block.sync
        def _(sp):
            sp.dma_start(A[:], P.rearrange("(t p) d -> p t d", p=CH)).then_inc(S["ld_P"], 16)
            sp.dma_start(cT[:], condT.rearrange("(t p) b -> p t b", p=CH)).then_inc(S["ld_cond"], 16)
            sp.dma_start(wad[:], w_adaln.rearrange("(t p) n -> p t n", p=CH)).then_inc(S["ld_wad"], 16)
            sp.dma_start(bad[:], b_adaln.rearrange("(o n) -> o n", o=1)).then_inc(S["ld_wad"], 16)
            for k, s in enumerate((0, 1, 3, 4)):
                for r in range(3):
                    sp.dma_start(wad2[:, :, k, 32 * r:32 * r + 32],
                                 w_adaln[:, s * C + 256:(s + 1) * C].rearrange("(t p) n -> p t n", p=CH)).then_inc(S["ld_wad"], 16)
                    sp.dma_start(bad2[:, k, 32 * r:32 * r + 32],
                                 b_adaln[s * C + 256:(s + 1) * C].rearrange("(o n) -> o n", o=1)).then_inc(S["ld_wad"], 16)
            def load_wt(n):
                sp.dma_start(wts[:, n % 4], WT[:, n * 512:(n + 1) * 512].rearrange("(t p) n -> p t n", p=CH))\
                    .then_inc(ld_wt[n % 4], 16)

            for n in range(4):
                load_wt(n)
            sp.dma_start(bUs[:], bU).then_inc(S["ld_bU"], 16)
            sp.dma_start(wqr[:, 0:2, :], w_qkv[0:256, :].rearrange("(t p) n -> p t n", p=128)).then_inc(S["ld_wq"], 16)
            sp.dma_start(wgr[:, 0:2, :], w_gate[0:256, :].rearrange("(t p) n -> p t n", p=128)).then_inc(S["ld_wq"], 16)
            for r in range(3):
                sp.dma_start(wqr[32 * r:32 * r + 32, 2, :], w_qkv[256:C, :]).then_inc(S["ld_wq"], 16)
                sp.dma_start(wgr[32 * r:32 * r + 32, 2, :], w_gate[256:C, :]).then_inc(S["ld_wq"], 16)
            sp.dma_start(wp[:], w_proj.rearrange("(t p) n -> p t n", p=CH)).then_inc(S["ld_misc"], 16)
            sp.dma_start(b2s[:], b2).then_inc(S["ld_misc"], 16)
            for m in range(MT):
                sp.dma_start(bqk[0:MROWS[m], m:m + 1],
                             b_qkv[m * HP * HD:m * HP * HD + MROWS[m]].rearrange("(p o) -> p o", o=1)).then_inc(S["ld_misc"], 16)
            sp.dma_start(bv[:], b_qkv[2 * C:3 * C].partition_broadcast(128)).then_inc(S["ld_misc"], 16)
            sp.dma_start(bp[:], b_proj.partition_broadcast(128)).then_inc(S["ld_misc"], 16)
            sp.wait_ge(S["mods"], 8)
            sp.dma_start(mod_d.rearrange("b p k -> p b k"), modt[:]).then_inc(S["mod_out"], 16)
            for b in range(NB):
                sp.wait_ge(S["gates"], 2 * b + 2)
                sp.dma_start(gate_d[b:b + 1], gts[:, b % 2]).then_inc(gate_out[b % 2], 16)
            for n in range(4, 8):
                sp.wait_ge(S["p_vf"], n - 3)
                load_wt(n)
            sp.wait_ge(S["vf_ready"], 8)
            sp.dma_start(up_d.rearrange("b i j -> b (i j)"), vf[:]).then_inc(S["vf_out"], 16)
            sp.wait_ge(S["vf_out"], 16)
            sp.dma_start(Ab[:], up_d.rearrange("b i j -> i b j")).then_inc(S["up_in"], 16)
            sp.wait_ge(S["rot_ready"], 8)
            sp.dma_start(rot_d.rearrange("b d n -> d b n"), Gs[:]).then_inc(S["rot_out"], 16)
            sp.wait_ge(S["rot_out"], 16)
            sp.wait_ge(S["mod_out"], 16)
            for k in range(2):
                sp.wait_ge(gate_out[k], 16 * NB // 2)
            sp.wait_ge(S["wq_split"], 5)

            def load_front(i):
                if not (isinstance(i, int) and i == 0):
                    wait_apart(sp, S["xrot"], i * NT)
                    sp.wait_ge(S["xT_ps"], i * 3)
                    sp.wait_ge(S["delta_ps"], i * NT)
                    wait_apart(sp, S["hF"], i * 3)
                sp.dma_start(xin[:], x[i].rearrange("(t p) c -> p t c", p=128)).then_inc(S["ld_x"], 16)
                sp.dma_start(rot[:], rot_d[i]).then_inc(S["ld_rot"], 16)
                sp.dma_start(modf[:], mod_d[i]).then_inc(S["ld_modf"], 16)

            def load_tail(i):
                if not (isinstance(i, int) and i == 0):
                    wait_apart(sp, S["nF"], i * 3)
                    wait_apart(sp, S["b2g"], i * NT)
                sp.dma_start(modn[:], mod_d[i]).then_inc(S["ld_modn"], 16)
                sp.dma_start(gat[:], gate_d[i].partition_broadcast(128)).then_inc(S["ld_gat"], 16)

            def store_parts(i):
                for m in range(MT):
                    wait_apart(sp, S["qkl"], i * MT + m + 1)
                    n = MROWS[m] // HD
                    for p in range(NPART):
                        sp.dma_start(qk_d[m * HP:m * HP + n, p], prt[0:MROWS[m], m % 2, p, :]).then_inc(parts_out[m % 2], 16)

            def load_quad(i, q):
                if q == 0:
                    sp.wait_ge(parts_out[0], parts_stored(i, 4))
                    wait_apart(sp, parts_out[1], parts_stored(i, 3))
                if not (isinstance(i, int) and i == 0):
                    wait_apart(sp, S["st_ps"], (i - 1) * 32 + 8 * q + 8)
                h = 4 * q
                for stack, base, groups in ((Ks, NH, ((0, 3, 0), (3, 2, 0), (5, 1, 0))), (Qs, 0, None)):
                    if groups:
                        for g, n, p in groups:
                            src = qk_d[base + h:base + h + 4, p:p + n].rearrange("h p d t -> (p d) h t")
                            sp.dma_start(stack[g * HD:(g + n) * HD, h:h + 4, :], src).then_inc(qin[q], 16)
                    else:
                        for g, p in enumerate((0, 0, 0, 1, 1, 2)):
                            src = qk_d[base + h:base + h + 4, p].rearrange("h d t -> d h t")
                            sp.dma_start(stack[g * HD:(g + 1) * HD, h:h + 4, :], src).then_inc(qin[q], 16)

            def load_max(i, q):
                wait_apart(sp, S["mT_sb"], i * 4 + q + 1)
                sp.dma_start(Qs[KROWS:KROWS + NPART, 4 * q:4 * q + 4, :], mTs[:, q % 2, :]).then_inc(m_in[q % 2], 16)

            def store_xn(i):
                sp.wait_ge(S["nHi"], i * 4 + 4)
                wait_apart(sp, S["nLo"], i * 2 + 2)
                sp.dma_start(xn_d[i, :, 0:2, :], Nh[:, 0:2, :].bitcast(F32)).then_inc(S["xn_out"], 16)
                sp.dma_start(xn_d[i, :, 2:4, :], Nl[:].bitcast(F32)).then_inc(S["xn_out"], 16)
                sp.dma_start(xn_d[i, 0:STACK, 4, :], Nh[0:STACK, 2, :].bitcast(F32)).then_inc(S["xn_out"], 16)

            load_front(0)
            store_parts(0)
            for q in range(4):
                load_quad(0, q)

            def sequence(i, first=False, second=False, last=False):
                if not last:
                    load_front(i + 1)
                if not first:
                    load_quad(i, 2)
                load_max(i, 0)
                if not first:
                    load_quad(i, 3)
                    load_tail(i - 1)
                load_max(i, 1)
                load_max(i, 2)
                if not last:
                    store_parts(i + 1)
                    load_quad(i + 1, 0)
                load_max(i, 3)
                if not last:
                    load_quad(i + 1, 1)
                if not first:
                    store_xn(i - 1)

            sequence(0, first=True)
            sequence(1, second=True)
            with sp.Fori(2, NB - 1) as i:
                sequence(i)
            sequence(NB - 1, last=True)
            load_tail(NB - 1)
            store_xn(NB - 1)
            sp.wait_ge(S["xn_out"], NB * 48)
            sp.wait_ge(S["x2_2"], NB * NT)
            sp.dma_start(b1s[:], b1T).then_inc(S["ld_b1"], 16)

            def load_expert(e):
                for t in range(HT):
                    if not (isinstance(e, int) and e == 0):
                        wait_apart(sp, S["w_hi"], e * HT * 2)
                        wait_apart(sp, S["w_lo"], e * HT * 3)
                    cols = slice(t * 128, (t + 1) * 128)
                    sp.dma_start(wr[:, t, 0:2, :], w1[e, 0:256, cols].rearrange("(c p) n -> p c n", p=128)).then_inc(wraw[t], 16)
                    for r in range(3):
                        sp.dma_start(wr[32 * r:32 * r + 32, t, 2, :], w1[e, 256:C, cols]).then_inc(wraw[t], 16)
                    sp.dma_start(vr[:, t, :], w2[e, cols, :]).then_inc(wraw[t], 16)

            def group_loads(e, pair, u, peeled=False):
                b = pair * 2 + u
                if not peeled:
                    g1 = e * NB + pair * 2 + (u - 1)
                    wait_apart(sp, S["m1_ps"], g1 * HT)
                    wait_apart(sp, S["eg"], g1 * NT)
                sp.dma_start(xn[:, u, 0:4, :].bitcast(F32), xn_d[b, :, 0:4, :]).then_inc(ld_xn[u], 16)
                sp.dma_start(xn[0:STACK, u, 4, :].bitcast(F32), xn_d[b, 0:STACK, 4, :]).then_inc(ld_xn[u], 16)
                sp.dma_start(gc[:, u, :], gate_d[b, 1, :].partition_broadcast(128)).then_inc(ld_gc[u], 16)

            load_expert(0)
            group_loads(0, 0, 0, peeled=True)
            group_loads(0, 0, 1, peeled=True)
            load_expert(1)
            with sp.Fori(1, NB // 2) as p:
                for u in range(2):
                    group_loads(0, p, u)
            with sp.Fori(1, NE - 1) as e:
                with sp.Fori(0, NB // 2) as p:
                    for u in range(2):
                        group_loads(e, p, u)
                load_expert(e + 1)
            with sp.Fori(0, NB // 2) as p:
                for u in range(2):
                    group_loads(NE - 1, p, u)
            with sp.Fori(0, NB) as b:
                wait_apart(sp, S["acc"], ((NE - 1) * NB) * NT + (b + 1) * NT)
                sp.dma_start(out[b].rearrange("(t p) c -> p t c", p=128), X2[:, b]).then_inc(yout, 16)
            sp.wait_ge(yout, NB * 16)

        @block.gpsimd
        def _(pool):
            chain = [0]

            def link(ins):
                chain[0] += 1
                ins.then_inc(S["pch"], 1)
                pool.wait_ge(S["pch"], chain[0])

            link(pool.memset(ident[:], 0.0))
            link(pool.affine_select(out=ident[:], in_=ident[:], compare_op=ALU.not_equal, fill=1.0, base=0,
                                    pattern=[[-1, 128]], channel_multiplier=1))
            link(pool.tensor_copy(identb[:], ident[:]))
            link(pool.memset(ones[:], 1.0))
            link(pool.memset(nhalf[:], -0.5))
            link(pool.memset(modt[:], 0.0))
            link(pool.memset(maskge[:], 1.0))
            link(pool.affine_select(out=maskge[:], in_=maskge[:], compare_op=ALU.is_ge, fill=0.0, base=0,
                                    pattern=[[-1, D]], channel_multiplier=1))
            link(pool.memset(striu[:], 1.0))
            link(pool.affine_select(out=striu[:], in_=striu[:], compare_op=ALU.is_gt, fill=0.0, base=0,
                                    pattern=[[1, D]], channel_multiplier=-1))
            for t in range(NSQ):
                pool.memset(pw[:, 0, t:t + 1], 2.0 ** t).then_inc(S["pch"], 1)
                pool.memset(pw[:, 1, t:t + 1], 2.0 ** -(t + 1)).then_inc(S["pch"], 1)
            chain[0] += 2 * NSQ
            pool.wait_ge(S["pch"], chain[0])
            pool.memset(sc[:, 15:16], 0.0).then_inc(S["const"], 1)
            pool.wait_ge(S["s_silu"], 2)
            pool.tensor_tensor(sT[:], cT[:], eT[:], ALU.mult).then_inc(S["s_silu"], 1)
            pool.wait_ge(S["ld_wq"], 128)
            pool.tensor_copy(wqh[:, 0:2, :], wqr[:, 0:2, :]).then_inc(S["wq_split"], 1)
            pool.tensor_copy(wqh[0:STACK, 2, :], wqr[0:STACK, 2, :]).then_inc(S["wq_split"], 1)
            pool.tensor_copy(wgh[:, 0:2, :], wgr[:, 0:2, :]).then_inc(S["wq_split"], 1)
            pool.tensor_copy(wgh[0:STACK, 2, :], wgr[0:STACK, 2, :]).then_inc(S["wq_split"], 1)
            pool.wait_ge(S["wq_split"], 4)
            link(pool.tensor_tensor(wql[:], wqr[:, 0:2, :], wqh[:, 0:2, :].bitcast(F32), ALU.subtract))
            link(pool.tensor_tensor(wgl[:], wgr[:, 0:2, :], wgh[:, 0:2, :].bitcast(F32), ALU.subtract))
            link(pool.tensor_tensor(wqh[64:96, 2, :], wqr[64:96, 2, :], wqh[64:96, 2, :].bitcast(F32), ALU.subtract))
            pool.tensor_tensor(wgh[64:96, 2, :], wgr[64:96, 2, :], wgh[64:96, 2, :].bitcast(F32), ALU.subtract)\
                .then_inc(S["wq_split"], 1)
            pool.wait_ge(S["up_in"], 16)
            pool.wait_ge(S["ld_bU"], 16)
            pool.tensor_tensor(Ab[:], Ab[:], bc(bUs[:].unsqueeze(1), [D, NB, D]), ALU.add).then_inc(S["expm_pool"], 1)
            pool.wait_ge(S["expm_dve"], FLAGS_DONE)
            pool.tensor_tensor(dg[:], bc(ident[0:NB, 0:NB].unsqueeze(2), [NB, NB, NSQ + 1]),
                               bc(fs[:].unsqueeze(1), [NB, NB, NSQ + 1]), ALU.mult).then_inc(S["expm_pool"], 1)
            pool.wait_ge(S["expm_act"], FLAGS_SPREAD)
            pool.tensor_scalar(omf[:], fsb[:, :, 0:NSQ], -1.0, 1.0, ALU.mult, ALU.add).then_inc(S["expm_pool"], 1)
            pool.wait_ge(S["expm_pool"], OMF_DONE)
            for t in range(NSQ):
                if t:
                    pool.wait_ge(S["p_sq"], 2 * t)
                link(pool.tensor_tensor(gI[:], bc(ident[0:D, 0:D].unsqueeze(1), [D, NB, D]),
                                        bc(omf[:, :, t:t + 1], [D, NB, D]), ALU.mult))
                if t == 0:
                    pool.wait_ge(S["expm_dve"], R_DONE)
                    pool.wait_ge(S["expm_act"], RT_DONE)
                else:
                    pool.wait_ge(S["sq_ready"], 2 * t)
                pool.tensor_tensor(L[:], RR[:], bc(fsb[:, :, t:t + 1], [D, NB, D]), ALU.mult).then_inc(S["pch"], 1)
                pool.tensor_tensor(LT[:], RT[:], bc(fsb[:, :, t:t + 1], [D, NB, D]), ALU.mult).then_inc(S["pch"], 1)
                chain[0] += 2
                pool.wait_ge(S["pch"], chain[0])
                pool.tensor_tensor(L[:], L[:], gI[:], ALU.add).then_inc(S["lr_ready"], 1)
                pool.tensor_tensor(LT[:], LT[:], gI[:], ALU.add).then_inc(S["lr_ready"], 1)
            pool.wait_ge(S["sq_ready"], 2 * NSQ)
            pool.wait_ge(S["p_sq"], 2 * NSQ)
            pool.tensor_tensor(RT[:], RT[:], bc(ident[0:D, 0:D].unsqueeze(1), [D, NB, D]), ALU.subtract).then_inc(S["rotm"], 1)
            pool.wait_ge(S["rot_out"], 16)
            pool.wait_ge(S["mod_out"], 16)
            for k in range(2):
                pool.wait_ge(gate_out[k], 16 * NB // 2)
            pool.wait_ge(S["p_rot"], NB)
            pool.memset(Ks[96:128], 1.0).then_inc(S["kones"], 1)
            pool.wait_ge(S["kones"], 1)
            pool.memset(Va[:, :, :, HD:HD + 1], 1.0).then_inc(S["vones"], 1)
            pool.wait_ge(S["vones"], 1)
            pool.memset(Va[:, :, :, HD + 1:VW], 0.0).then_inc(S["vones"], 1)

            def eps_pow(i, k, mean_sem, out_sem, chain_sem):
                wait_apart(pool, mean_sem, i * NT + NT)
                pool.tensor_scalar(ve[:, k], mv[:, k, :, 1], 1.0, 1e-6, ALU.mult, ALU.add).then_inc(chain_sem, 1)
                wait_apart(pool, chain_sem, i + 1)
                pool.tensor_tensor(rstd[:, k], ve[:, k], nhalf[:], ALU.pow).then_inc(out_sem, 1)

            def split_front(i):
                for c in range(3):
                    rows = 128 if c < 2 else STACK
                    wait_apart(pool, S["hF"], i * 3 + c + 1)
                    if c == 0 and not fixed(i, 0):
                        wait_apart(pool, S["v_ps"], i * NT)
                    pool.tensor_copy(Hh[0:rows, c, :], F[0:rows, c, :]).then_inc(S["hHi"], 1)
                pool.wait_ge(S["hHi"], i * 4 + 3)
                pool.tensor_tensor(Hh[32:64, 2, :], F[32:64, 2, :], Hh[32:64, 2, :].bitcast(F32), ALU.subtract)\
                    .then_inc(S["hHi"], 1)

            def last_parts(i):
                for m in range(MT):
                    pool.wait_ge(S["qkm"], i * MT + m + 1)
                    pool.tensor_tensor(prt[0:MROWS[m], m % 2, 2, :], QF[0:MROWS[m], m % 2, :],
                                       prt[0:MROWS[m], m % 2, 1, :], ALU.subtract).then_inc(S["qkl"], 1)

            def split_tail(i):
                for c in range(3):
                    rows = 128 if c < 2 else STACK
                    wait_apart(pool, S["nF"], i * 3 + c + 1)
                    if c == 0 and not fixed(i, 0):
                        pool.wait_ge(S["xn_out"], i * 48)
                        wait_apart(pool, S["gl_ps"], i)
                    pool.tensor_copy(Nh[0:rows, c, :], F[0:rows, c, :]).then_inc(S["nHi"], 1)
                pool.wait_ge(S["nHi"], i * 4 + 3)
                pool.tensor_tensor(Nh[32:64, 2, :], F[32:64, 2, :], Nh[32:64, 2, :].bitcast(F32), ALU.subtract)\
                    .then_inc(S["nHi"], 1)

            def sequence(i, first=False, second=False, last=False):
                if not last:
                    eps_pow(i + 1, 0, S["mvf"], S["rstd_f"], S["var_eps"])
                    split_front(i + 1)
                    last_parts(i + 1)
                if not first:
                    eps_pow(i - 1, 1, S["mvn"], S["rstd_n"], S["var_eps2"])
                    split_tail(i - 1)

            eps_pow(0, 0, S["mvf"], S["rstd_f"], S["var_eps"])
            split_front(0)
            last_parts(0)
            sequence(0, first=True)
            sequence(1, second=True)
            with pool.Fori(2, NB - 1) as i:
                sequence(i)
            sequence(NB - 1, last=True)
            eps_pow(NB - 1, 1, S["mvn"], S["rstd_n"], S["var_eps2"])
            split_tail(NB - 1)
            pool.wait_ge(S["xn_out"], NB * 48)
            pool.wait_ge(S["x2_2"], NB * NT)

            def split_expert(e):
                for t in range(HT):
                    wait_apart(pool, wraw[t], e * 80 + 80)
                    if not (isinstance(e, int) and e == 0):
                        wait_apart(pool, S["m2_ps"], (e * NB - 1) * HT + (t + 1))
                    pool.tensor_copy(w1h[:, t, 0:2, :], wr[:, t, 0:2, :]).then_inc(S["w_hi"], 1)
                    pool.tensor_copy(w1h[0:STACK, t, 2, :], wr[0:STACK, t, 2, :]).then_inc(S["w_free"], 1)
                    pool.tensor_copy(w2h[:, t, :], vr[:, t, :]).then_inc(S["w_hi"], 1)
                    pool.wait_ge(S["w_hi"], e * (2 * HT) + (2 * t + 2))
                    pool.wait_ge(S["w_free"], e * HT + (t + 1))
                    pool.tensor_tensor(w1l[:, t], wr[:, t, 0:2, :], w1h[:, t, 0:2, :].bitcast(F32), ALU.subtract)\
                        .then_inc(S["w_lo"], 1)
                    pool.wait_ge(S["w_lo"], e * (3 * HT) + (3 * t + 1))
                    pool.tensor_tensor(w1h[64:96, t, 2, :], wr[64:96, t, 2, :], w1h[64:96, t, 2, :].bitcast(F32),
                                       ALU.subtract).then_inc(S["w_lo"], 1)
                    pool.wait_ge(S["w_lo"], e * (3 * HT) + (3 * t + 2))
                    pool.tensor_tensor(w2l[:, t, :], vr[:, t, :], w2h[:, t, :].bitcast(F32), ALU.subtract)\
                        .then_inc(S["w_lo"], 1)

            split_expert(0)
            with pool.Fori(1, NE) as e:
                split_expert(e)

        @block.scalar
        def _(act):
            act.wait_ge(S["ld_cond"], 16)
            act.activation(eT[:], cT[:], ACT.Exp, scale=-1.0).then_inc(S["e_silu"], 1)

            def side(k):
                if k == 2:
                    act.wait_ge(S["p_mods"], 1)
                    for s in range(4):
                        for c, rows in ((slice(0, 2), 128), (slice(2, 3), STACK)):
                            n = c.stop - c.start
                            src = bank[2][0:rows, s * 24 + c.start * 8:s * 24 + c.stop * 8].rearrange("p (c b) -> p c b", b=NB)
                            dst = modt[0:rows, :, 3 * s + c.start:3 * s + c.stop].rearrange("p b c -> p c b")
                            act.activation(dst, src, ACT.Copy, bias=float(s % 2)).then_inc(S["mods"], 1)
                if 3 <= k < 3 + NB:
                    b = k - 3
                    for g in range(2):
                        act.wait_ge(S["p_gates"], 2 * b + g + 1)
                        if b >= 2 and g == 0:
                            act.wait_ge(gate_out[b % 2], 16 * (b // 2))
                        act.activation(gts[:, b % 2, g, :], bank[2 + g][0:1, 0:C], ACT.Copy).then_inc(S["gates"], 1)
                if 12 <= k < 20:
                    n = k - 12
                    act.wait_ge(S["p_vf"], n + 1)
                    act.activation(vf[:, n * 512:(n + 1) * 512], bank[2 + n % 2][0:NB, :], ACT.Copy).then_inc(S["vf_ready"], 1)
                if k == 24:
                    act.wait_ge(S["expm_ps"], PS_FS)
                    act.activation(fsb[:], bank[4][0:D, 0:NB * (NSQ + 1)].rearrange("p (b t) -> p b t", b=NB),
                                   ACT.Copy).then_inc(S["expm_act"], 1)
                if k == 26:
                    act.wait_ge(S["expm_ps"], PS_A2)
                    act.activation(A2[:], bank[2][0:D].rearrange("p (b j) -> p b j", b=NB), ACT.Copy, scale=-1.0)\
                        .then_inc(S["expm_act"], 1)
                if k == 27:
                    act.wait_ge(S["expm_ps"], PS_A3)
                    act.activation(A3[:], bank[3][0:D].rearrange("p (b j) -> p b j", b=NB), ACT.Copy)\
                        .then_inc(S["expm_act"], 1)
                    act.wait_ge(S["expm_ps"], PS_A4)
                    act.activation(A4[:], bank[4][0:D].rearrange("p (b j) -> p b j", b=NB), ACT.Copy)\
                        .then_inc(S["expm_act"], 1)
                if k == 30:
                    act.wait_ge(S["expm_ps"], PS_RT)
                    act.activation(RT[:], bank[4][0:D].rearrange("p (b j) -> p b j", b=NB), ACT.Copy)\
                        .then_inc(S["expm_act"], 1)
                if 31 <= k < 31 + 2 * NSQ:
                    t, half = (k - 31) // 2, (k - 31) % 2
                    act.wait_ge(S["p_sq"], 2 * t + half + 1)
                    if half == 1:
                        for dst, src in ((RR, bank[2]), (RT, bank[3])):
                            act.activation(dst[:], src[0:D].rearrange("p (b j) -> p b j", b=NB), ACT.Copy)\
                                .then_inc(S["sq_ready"], 1)

            for j in range(D):
                act.wait_ge(S["qrD"], j + 1)
                act.activation(sc[:, 0:1], R[0][0:CH, j:j + 1], ACT.Sqrt).then_inc(S["sigma"], 1)
                side(j)
            act.wait_ge(S["expm_ps"], PS_VT)
            act.activation(VT[:], bank[2][0:D, 0:C], ACT.Copy).then_inc(S["expm_act"], 1)
            act.wait_ge(S["expm_ps"], PS_XT)
            act.activation(XX[:, 1, :], bank[3][0:D, 0:D], ACT.Copy).then_inc(S["XT_ready"], 1)
            for k in range(5):
                act.wait_ge(S["p_X"], k + 1)
                act.activation(XX[:], bank[4][0:D, 0:2 * D].rearrange("p (k j) -> p k j", k=2), ACT.Copy)\
                    .then_inc(S["XT_ready"], 1)
            for b in range(NB):
                act.wait_ge(S["p_rot"], b + 1)
                act.activation(Gs[:, b, :], bank[b][0:D, 0:C], ACT.Copy).then_inc(S["rot_ready"], 1)

            act.wait_ge(S["rot_out"], 16)
            act.wait_ge(S["ld_misc"], 16 * (4 + MT))
            act.wait_ge(S["wq_split"], 5)

            def xT_out(i):
                for c in range(NCH):
                    act.wait_ge(S["xT_ps"], i * 3 + c + 1)
                    act.activation(xT[:, c, :], R[c % 2][0:CH, :], ACT.Copy).then_inc(S["xT_sb"], 1)

            def z_out(i):
                act.wait_ge(S["z_ps"], i + 1)
                act.activation(zT[:], R[1][0:D, :], ACT.Copy).then_inc(S["z_sb"], 1)

            def hT_out(i, nosplit=False):
                act.wait_ge(S["ld_modf"], i * 16 + 16)
                for c in range(3):
                    rows = 128 if c < 2 else STACK
                    act.wait_ge(S["hT_ps"], i * 3 + c + 1)
                    if c == 0 and not fixed(i, 0):
                        act.wait_ge(S["hHi"], i * 4)
                        act.wait_ge(S["hLo"], i * 2)
                        if not fixed(i, 1):
                            act.wait_ge(S["nHi"], (i - 2) * 4)
                            act.wait_ge(S["nLo"], (i - 2) * 2)
                    act.activation(F[0:rows, c, :], R[c % 2][0:rows, :], ACT.Identity, scale=modf[0:rows, 3 + c:4 + c],
                                   bias=modf[0:rows, c:c + 1]).then_inc(S["hF"], 1)

            def qk_out(i):
                for m in range(MT):
                    rows = MROWS[m]
                    act.wait_ge(S["qk_ps"], i * MT + m + 1)
                    if m >= 2:
                        act.wait_ge(S["qkl"], i * MT + (m - 1))
                        act.wait_ge(parts_out[m % 2], parts_stored(i, m - 2))
                    elif not fixed(i, 0):
                        act.wait_ge(S["qkl"], i * MT)
                        act.wait_ge(parts_out[m % 2], parts_stored(i - 1, 4 - m % 2))
                    src = R[(m + 1) % 2][0:rows, :]
                    act.activation(QF[0:rows, m % 2, :], src, ACT.Identity, bias=bqk[0:rows, m:m + 1]).then_inc(S["qkF"], 1)
                    act.activation(prt[0:rows, m % 2, 0, :], src, ACT.Identity, bias=bqk[0:rows, m:m + 1])\
                        .then_inc(S["qkh"], 1)

            def mT_out(i, q):
                act.wait_ge(S["mT_ps"], i * 4 + q + 1)
                if q >= 2 or not fixed(i, 0):
                    act.wait_ge(m_in[q % 2], (i * 2 + q // 2) * 16)
                act.activation(mTs[:, q % 2, :], R[0][0:48, 0:64].bitcast(BF16), ACT.Copy).then_inc(S["mT_sb"], 1)

            def exps(i, h):
                for k in range(2):
                    act.wait_ge(S["st_ps"], i * 32 + (2 * h + k + 1))
                    if h >= 2 or not fixed(i, 0):
                        act.wait_ge(S["av_ps"], i * 32 + (2 * (h - 2) + k + 1))
                    act.activation(PT[:, h % 2, 2 * k:2 * k + 2, :], ST[k][:], ACT.Exp, scale=SCALE)\
                        .then_inc(S["expd"], 1)

            def av_out(i, h):
                act.wait_ge(S["av_ps"], i * 32 + (2 * h + 2))
                if h or not fixed(i, 0):
                    act.wait_ge(S["tok_ps"], i * NH + h)
                act.activation(oTh[:], OB[0][0:VW, :], ACT.Copy).then_inc(S["avT"], 1)

            def oT_out(i):
                for c in range(NCH):
                    act.wait_ge(S["oT_ps"], i * 3 + c + 1)
                    act.activation(xT[:, c, :], R[c % 2][0:CH, :], ACT.Copy).then_inc(S["oT_sb"], 1)

            def nT_out(i):
                act.wait_ge(S["ld_modn"], i * 16 + 16)
                for c in range(3):
                    rows = 128 if c < 2 else STACK
                    act.wait_ge(S["nT_ps"], i * 3 + c + 1)
                    if c == 0:
                        act.wait_ge(S["nHi"], i * 4)
                        act.wait_ge(S["nLo"], i * 2)
                        fronts = i + 3 if not isinstance(i, int) else min(i + 3, NB)
                        act.wait_ge(S["hHi"], fronts * 4)
                        act.wait_ge(S["hLo"], fronts * 2)
                    act.activation(F[0:rows, c, :], R[c % 2][0:rows, :], ACT.Identity,
                                   scale=modn[0:rows, 9 + c:10 + c], bias=modn[0:rows, 6 + c:7 + c]).then_inc(S["nF"], 1)

            def gate_exp(i):
                act.wait_ge(S["top"], i + 1)
                act.activation(m12[:, 3, :], m12[:, 2, :], ACT.Exp).then_inc(S["g_exp"], 1)

            def cwT_out(i):
                act.wait_ge(S["cwT_ps"], i + 1)
                act.activation(zT[0:NE, :], R[0][0:NE, :], ACT.Copy).then_inc(S["cwT_sb"], 1)

            def sequence(i, first=False, second=False, last=False):
                for h in range(NH):
                    if h == 4 and not (first or second):
                        cwT_out(i - 2)
                    if h < 8 and not first:
                        exps(i - 1, h + 8)
                    if h >= 8:
                        exps(i, h - 8)
                    if h >= 10:
                        av_out(i, h - 10)
                    elif not first:
                        av_out(i - 1, h + 6)
                    if h == 2 and not (first or second):
                        gate_exp(i - 2)
                    if h == 8 and not last:
                        xT_out(i + 1)
                    if h == 9 and not last:
                        z_out(i + 1)
                    if h == 11:
                        if not last:
                            hT_out(i + 1)
                        if not first:
                            oT_out(i - 1)
                    if h == 12 and not last:
                        qk_out(i + 1)
                    if h == 15 and not first:
                        nT_out(i - 1)
                    if h % 4 == 3:
                        mT_out(i, h // 4)

            xT_out(0)
            z_out(0)
            hT_out(0)
            qk_out(0)
            sequence(0, first=True)
            sequence(1, second=True)
            with act.Fori(2, NB - 1) as i:
                sequence(i)
            sequence(NB - 1, last=True)
            for h in range(8, NH + 2):
                if h == 12:
                    cwT_out(NB - 2)
                if h < NH:
                    exps(NB - 1, h)
                av_out(NB - 1, h - 2)
                if h == 10:
                    gate_exp(NB - 2)
            oT_out(NB - 1)
            nT_out(NB - 1)
            gate_exp(NB - 1)
            cwT_out(NB - 1)
            act.wait_ge(S["x2_2"], NB * NT)
            act.wait_ge(S["xn_out"], NB * 48)
            act.wait_ge(S["ld_b1"], 16)

            def gelus(e, g, later):
                for t in range(HT):
                    act.wait_ge(S["m1_ps"], g * HT + (t + 1))
                    if later or t >= 3:
                        act.wait_ge(S["ghi"], g * HT + (t - 2))
                        act.wait_ge(S["glo"], g * HT + (t - 2))
                    act.activation(GF[:, t % 3, :], m1_bank(t),
                                   ACT.Gelu_apprx_tanh, bias=b1s[:, e * HT + t:e * HT + t + 1] if isinstance(e, int)
                                   else b1s[:, bass.ds(e * HT + t, 1)]).then_inc(S["gelu"], 1)
                    act.wait_ge(S["gelu"], g * HT + (t + 1))
                    if later or t >= 3:
                        act.wait_ge(S["m2_ps"], g * HT + (t - 2))
                    act.activation(Gh[:, t % 3, :], GF[:, t % 3, :], ACT.Copy).then_inc(S["ghi"], 1)

            gelus(0, 0, False)
            with act.Fori(1, NB) as g:
                gelus(0, g, True)
            with act.Fori(1, NE) as e:
                with act.Fori(0, NB) as b:
                    gelus(e, e * NB + b, True)

        @block.vector
        def _(v):
            chain = [0]

            def link(ins):
                chain[0] += 1
                ins.then_inc(S["dch"], 1)
                v.wait_ge(S["dch"], chain[0])

            v.wait_ge(S["const"], 1)
            v.wait_ge(S["e_silu"], 1)
            v.tensor_scalar(eT[:], eT[:], 1.0, None, ALU.add).then_inc(S["s_silu"], 1)
            v.wait_ge(S["s_silu"], 1)
            v.reciprocal(eT[:], eT[:]).then_inc(S["s_silu"], 1)

            I8 = bc(ident[0:D, 0:D].unsqueeze(1), [D, NB, D])

            def poly(k, dst):
                c = TAYLOR[4 * k:4 * k + 4]
                link(v.tensor_scalar(dst[:], A3[:], c[3], None, ALU.mult))
                link(v.scalar_tensor_tensor(dst[:], A2[:], c[2], dst[:], ALU.mult, ALU.add))
                link(v.scalar_tensor_tensor(dst[:], Ab[:], c[1], dst[:], ALU.mult, ALU.add))
                return v.scalar_tensor_tensor(dst[:], I8, c[0], dst[:], ALU.mult, ALU.add)

            def view8(b):
                return b[0:D].rearrange("p (b j) -> p b j", b=NB)

            def side(k):
                if k == 22:
                    v.wait_ge(S["expm_ps"], PS_UPT)
                    v.tensor_tensor(Ab[:], Ab[:], view8(bank[2]), ALU.subtract).then_inc(S["expm_dve"], 1)
                    v.wait_ge(S["expm_dve"], SKEW_DONE)
                    v.tensor_reduce(rs[:], Ab[:], AX.X, ALU.add, apply_absolute_value=True).then_inc(S["expm_dve"], 1)
                if k == 23:
                    v.wait_ge(S["expm_ps"], PS_RST)
                    link(v.tensor_reduce(nrm[:, 0:1], bank[3][0:NB, 0:D], AX.X, ALU.max))
                    link(v.tensor_scalar(fs[:, 0:NSQ], pw[:, 0, :], nrm[:, 0:1], None, ALU.is_lt))
                    link(v.tensor_tensor(fq[:], fs[:, 0:NSQ], pw[:, 1, :], ALU.mult))
                    link(v.tensor_reduce(nrm[:, 1:2], fq[:], AX.X, ALU.add))
                    v.tensor_scalar(fs[:, NSQ:NSQ + 1], nrm[:, 1:2], -1.0, 1.0, ALU.mult, ALU.add).then_inc(S["expm_dve"], 1)
                if k == 25:
                    v.wait_ge(S["expm_act"], FLAGS_SPREAD)
                    v.tensor_tensor(Ab[:], Ab[:], bc(fsb[:, :, NSQ:NSQ + 1], [D, NB, D]), ALU.mult).then_inc(S["expm_dve"], 1)
                if k == 28:
                    v.wait_ge(S["expm_act"], A3_DONE)
                    v.wait_ge(S["expm_act"], A2_DONE)
                    v.wait_ge(S["expm_dve"], SCALED_DONE)
                    poly(2, Bk).then_inc(S["expm_dve"], 1)
                    link(poly(1, L))
                    v.wait_ge(S["expm_ps"], PS_H1)
                    v.tensor_tensor(L[:], L[:], view8(bank[2]), ALU.add).then_inc(S["expm_dve"], 1)
                    link(poly(0, RR))
                if k == 29:
                    v.wait_ge(S["expm_ps"], PS_H2)
                    v.tensor_tensor(RR[:], RR[:], view8(bank[3]), ALU.add).then_inc(S["expm_dve"], 1)

            v.wait_ge(S["ld_P"], 16)
            v.tensor_tensor(a0m[:, 0:1], A[:, 0, 0:1], maskge[:, 0:1], ALU.mult).then_inc(S["a0"], 1)
            sig, g2, nb, u, vv, rc = (sc[:, k:k + 1] for k in range(6))
            for j in range(D):
                am = a0m[:, j % 2:j % 2 + 1]
                v.wait_ge(S["qrE"], j + 1)
                link(v.tensor_copy(Es[:, j:D], R[1][0:CH, j:D]))
                link(v.tensor_scalar(g2, Es[:, j:j + 1], 0.0, 2.0, ALU.is_ge, ALU.mult))
                v.wait_ge(S["sigma"], j + 1)
                link(v.scalar_tensor_tensor(nb, g2, -1.0, sig, ALU.add, ALU.mult))
                ins = v.scalar_tensor_tensor(u, Es[:, j:j + 1], 2.0, nb, ALU.mult, ALU.add)
                if j + 1 < D:
                    ins.then_inc(S["dch"], 1)
                    chain[0] += 1
                    v.scalar_tensor_tensor(t1[:, j + 1:D], Es[:, j + 1:D], nb, R[0][0:CH, j + 1:D], ALU.mult, ALU.add)\
                        .then_inc(S["dch"], 1)
                    chain[0] += 1
                    v.wait_ge(S["dch"], chain[0])
                else:
                    link(ins)
                link(v.scalar_tensor_tensor(vv, u, nb, R[0][0:CH, j:j + 1], ALU.mult, ALU.add))
                v.scalar_tensor_tensor(V0[:, j:j + 1], ident[0:CH, j:j + 1], nb, am, ALU.mult, ALU.add).then_inc(S["dch"], 1)
                chain[0] += 1
                link(v.reciprocal(rc, vv))
                if j + 1 < D:
                    link(v.tensor_scalar(cc[:, j + 1:D], t1[:, j + 1:D], rc, -2.0, ALU.mult, ALU.mult))
                    for t in (0, 1, 2):
                        vj = V0[:, j:j + 1] if t == 0 else A[:, t, j:j + 1]
                        v.scalar_tensor_tensor(A[:, t, j + 1:D], cc[:, j + 1:D], vj, A[:, t, j + 1:D],
                                               ALU.mult, ALU.add).then_inc(S["upd"], 1)
                    v.wait_ge(S["upd"], 3 * j + 1)
                    v.tensor_tensor(a0m[:, (j + 1) % 2:(j + 1) % 2 + 1], A[:, 0, j + 1:j + 2], maskge[:, j + 1:j + 2],
                                    ALU.mult).then_inc(S["a0"], 1)
                side(j)
            v.wait_ge(S["dch"], chain[0])
            v.tensor_copy(A[:, 0, :], V0[:]).then_inc(S["V_ready"], 1)
            v.wait_ge(S["expm_ps"], PS_S)
            link(v.tensor_tensor_reduce(out=Y[:], in0=R[0][0:D, 0:D], in1=ident[0:D, 0:D], scale=1.0, scalar=0.0,
                                        op0=ALU.mult, op1=ALU.add, accum_out=dd[:, 0:1]))
            link(v.reciprocal(dd[:, 1:2], dd[:, 0:1]))
            link(v.tensor_scalar(dd[:, 2:3], dd[:, 1:2], -2.0, None, ALU.mult))
            link(v.tensor_scalar(dd[:, 3:4], dd[:, 1:2], 2.0, None, ALU.mult))
            v.scalar_tensor_tensor(XX[:, 0, :], R[0][0:D, 0:D], dd[:, 2:3], striu[:], ALU.mult, ALU.mult)\
                .then_inc(S["expm_dve"], 1)
            v.wait_ge(S["expm_act"], VT_DONE)
            v.tensor_scalar(Y[:], VT[:, 0:D], dd[:, 3:4], None, ALU.mult).then_inc(S["Y_ready"], 1)
            for k in range(6):
                v.wait_ge(S["p_Y"], k + 1)
                v.tensor_tensor(Y[:], Y[:], bank[5][0:D, 0:D], ALU.add).then_inc(S["Y_ready"], 1)
            v.wait_ge(S["p_U"], 2)
            pu = bank[6][0:CH, 0:NCH * D].rearrange("p (t d) -> p t d", t=NCH)
            v.tensor_scalar(U[:, 1:NCH, :], pu[:, 1:NCH, :], -1.0, None, ALU.mult).then_inc(S["U_ready"], 1)
            v.scalar_tensor_tensor(U[:, 0, :], pu[:, 0, :], -1.0, ident[0:CH, 0:D], ALU.mult, ALU.add).then_inc(S["U_ready"], 1)
            v.tensor_scalar(UT[:, D:C], bank[7][0:D, D:C], -1.0, None, ALU.mult).then_inc(S["U_ready"], 1)
            v.scalar_tensor_tensor(UT[:, 0:D], bank[7][0:D, 0:D], -1.0, ident[0:D, 0:D], ALU.mult, ALU.add)\
                .then_inc(S["U_ready"], 1)

            v.wait_ge(S["rot_out"], 16)
            v.wait_ge(S["vones"], 2)

            def xrot(i):
                v.wait_ge(S["ld_x"], i * 16 + 16)
                for t in range(NT):
                    v.wait_ge(S["delta_ps"], i * NT + t + 1)
                    v.tensor_tensor(X2[:, i, t, :], R[t % 2][:, 0:C], xin[:, t, :], ALU.add).then_inc(S["xrot"], 1)
                    wait_apart(v, S["xrot"], i * NT + t + 1)
                    v.bn_stats(st6[:, 0, t, :], X2[:, i, t, :]).then_inc(S["bst"], 1)
                for t in range(NT):
                    wait_apart(v, S["bst"], i * NT + t + 1)
                    v.bn_aggr(mv[:, 0, t, :], st6[:, 0, t, :]).then_inc(S["mvf"], 1)

            def normalise(i, k, ready, done):
                v.wait_ge(ready, i + 1)
                for t in range(NT):
                    v.tensor_scalar(xh[:, t, 0:256], X2[:, i, t, 0:256], mv[:, k, t, 0:1], rstd[:, k, t:t + 1],
                                    ALU.subtract, ALU.mult).then_inc(done, 1)
                    last = X2[:, i, t, 256:C]
                    v.tensor_scalar(xh[:, t, 256:XW].rearrange("p (r n) -> p r n", r=3),
                                    bc(last.unsqueeze(1), [128, 3, 32]), mv[:, k, t, 0:1], rstd[:, k, t:t + 1],
                                    ALU.subtract, ALU.mult).then_inc(done, 1)

            def norm_front(i):
                if not fixed(i, 0):
                    v.wait_ge(S["hT_ps"], i * 3)
                    if not fixed(i, 1):
                        v.wait_ge(S["nT_ps"], (i - 2) * 3)
                normalise(i, 0, S["rstd_f"], S["xh_f1"])

            def h_lo(i):
                if not (isinstance(i, int) and i == 0):
                    v.wait_ge(S["v_ps"], i * NT)
                for c in range(2):
                    v.wait_ge(S["hHi"], i * 4 + c + 1)
                    v.tensor_tensor(Hl[:, c, :], F[:, c, :], Hh[:, c, :].bitcast(F32), ALU.subtract).then_inc(S["hLo"], 1)

            def qk_parts(i):
                for m in range(MT):
                    rows, s = MROWS[m], m % 2
                    v.wait_ge(S["qkF"], i * MT + m + 1)
                    v.wait_ge(S["qkh"], i * MT + m + 1)
                    v.tensor_tensor(QF[0:rows, s, :], QF[0:rows, s, :], prt[0:rows, s, 0, :], ALU.subtract)\
                        .then_inc(S["qkr"], 1)
                    v.wait_ge(S["qkr"], i * MT + m + 1)
                    v.tensor_copy(prt[0:rows, s, 1, :], QF[0:rows, s, :]).then_inc(S["qkm"], 1)

            def v_out(i):
                v.wait_ge(S["av_ps"], i * 32)
                for t in range(NT):
                    v.wait_ge(S["v_ps"], i * NT + t + 1)
                    v.tensor_tensor(Va[:, t, :, 0:HD], R[t % 2][:, 0:C].rearrange("p (h d) -> p h d", h=NH),
                                    bv[:].rearrange("p (h d) -> p h d", h=NH), ALU.add).then_inc(S["v_sb"], 1)

            def maxima(i, h):
                q, s = h // 4, h % 4
                for t in range(NT):
                    v.wait_ge(S["s_ps"], i * 64 + (4 * h + t + 1))
                    v.tensor_reduce(mx[:, q, s, t:t + 1], R[t % 2][:], AX.X, ALU.max, negate=True).then_inc(S["smax"], 1)

            def max_parts(i, q):
                v.wait_ge(S["smax"], i * 64 + 16 * (q + 1))
                if q:
                    v.wait_ge(S["mT_ps"], i * 4 + q)
                else:
                    v.wait_ge(S["mT_ps"], i * 4)
                m = mx[:, q].rearrange("p h t -> p (h t)")
                first = i * 16 + 4 * q
                v.tensor_copy(mp[:, 0, :], m).then_inc(S["mparts"], 1)
                v.wait_ge(S["mparts"], first + 1)
                v.tensor_tensor(mr[:], m, mp[:, 0, :], ALU.subtract).then_inc(S["mparts"], 1)
                v.wait_ge(S["mparts"], first + 2)
                v.tensor_copy(mp[:, 1, :], mr[:]).then_inc(S["mparts"], 1)
                v.wait_ge(S["mparts"], first + 3)
                v.tensor_tensor(mp[:, 2, :], mr[:], mp[:, 1, :], ALU.subtract).then_inc(S["mparts"], 1)

            def o_out(i, p):
                v.wait_ge(S["tok_ps"], i * NH + 2 * p + 2)
                src = tok
                v.reciprocal(rec[:, p % 2], src[:, :, :, HD]).then_inc(S["orec"], 1)
                v.wait_ge(S["orec"], i * 8 + p + 1)
                if p == 0:
                    v.wait_ge(S["oT_ps"], i * 3)
                v.tensor_tensor(o[:, :, 2 * p * HD:2 * (p + 1) * HD].rearrange("p t (s d) -> p t s d", s=2),
                                src[:, :, :, 0:HD], bc(rec[:, p % 2].unsqueeze(3), [128, NT, 2, HD]), ALU.mult)\
                    .then_inc(S["o_sb"], 1)

            def x2_attn(i):
                v.wait_ge(S["ld_gat"], i * 16 + 16)
                for t in range(NT):
                    v.wait_ge(S["proj_ps"], i * NT + t + 1)
                    v.tensor_tensor(yt[:, t % 2, :], R[t % 2][:, 0:C], bp[:], ALU.add).then_inc(S["yg"], 1)
                    v.wait_ge(S["yg"], i * 8 + 2 * t + 1)
                    v.tensor_tensor(yt[:, t % 2, :], yt[:, t % 2, :], gat[:, 0, :], ALU.mult).then_inc(S["yg"], 1)
                    v.wait_ge(S["yg"], i * 8 + 2 * t + 2)
                    v.tensor_tensor(X2[:, i, t, :], X2[:, i, t, :], yt[:, t % 2, :], ALU.add).then_inc(S["x2_1"], 1)
                    wait_apart(v, S["x2_1"], i * NT + t + 1)
                    v.bn_stats(st6[:, 1, t, :], X2[:, i, t, :]).then_inc(S["bst2"], 1)
                for t in range(NT):
                    wait_apart(v, S["bst2"], i * NT + t + 1)
                    v.bn_aggr(mv[:, 1, t, :], st6[:, 1, t, :]).then_inc(S["mvn"], 1)

            def norm_tail(i):
                v.wait_ge(S["nT_ps"], i * 3)
                fronts = i + 3 if not isinstance(i, int) else min(i + 3, NB)
                v.wait_ge(S["hT_ps"], fronts * 3)
                normalise(i, 1, S["rstd_n"], S["xh_n"])

            def n_lo(i):
                for c in range(2):
                    v.wait_ge(S["nHi"], i * 4 + c + 1)
                    v.tensor_tensor(Nl[:, c, :], F[:, c, :], Nh[:, c, :].bitcast(F32), ALU.subtract).then_inc(S["nLo"], 1)

            def seq(base, per):
                n = [0]

                def step(ins):
                    n[0] += 1
                    ins.then_inc(S["lgc"], 1)
                    v.wait_ge(S["lgc"], base * per + n[0])
                return step, n

            NLG = 20

            def first_of(step, mask, eq):
                step(v.tensor_copy(mask[:, :, 0:1], eq[:, :, 0:1]))
                step(v.tensor_scalar(us[:, :, 0:1], eq[:, :, 0:1], -1.0, 1.0, ALU.mult, ALU.add))
                for e in range(1, NE):
                    step(v.tensor_tensor(mask[:, :, e:e + 1], eq[:, :, e:e + 1], us[:, :, 0:1], ALU.mult))
                    if e + 1 < NE:
                        step(v.tensor_tensor(us[:, :, 0:1], us[:, :, 0:1], mask[:, :, e:e + 1], ALU.subtract))

            def top2(i):
                step, n = seq(i, NLG)
                v.wait_ge(S["gl_ps"], i + 1)
                step(v.tensor_copy(lg[:], R[0][:, 0:NT * NE].rearrange("p (t e) -> p t e", t=NT)))
                step(v.tensor_reduce(m12[:, 0, :], lg[:], AX.X, ALU.max))
                step(v.tensor_tensor(l2[:], lg[:], bc(m12[:, 0, :].unsqueeze(2), [128, NT, NE]), ALU.is_equal))
                first_of(step, k1, l2)
                step(v.scalar_tensor_tensor(l2[:], k1[:], -3.0e38, lg[:], ALU.mult, ALU.add))
                step(v.tensor_reduce(m12[:, 1, :], l2[:], AX.X, ALU.max))
                step(v.tensor_tensor(l2[:], l2[:], bc(m12[:, 1, :].unsqueeze(2), [128, NT, NE]), ALU.is_equal))
                first_of(step, k2, l2)
                v.tensor_tensor(m12[:, 2, :], m12[:, 1, :], m12[:, 0, :], ALU.subtract).then_inc(S["top"], 1)
                assert n[0] == NLG

            def weights(i):
                v.wait_ge(S["g_exp"], i + 1)
                w = S["cw_ready"]
                v.tensor_scalar(m12[:, 0, :], m12[:, 3, :], 1.0, None, ALU.add).then_inc(w, 1)
                v.wait_ge(w, i * 6 + 1)
                v.reciprocal(m12[:, 1, :], m12[:, 0, :]).then_inc(w, 1)
                v.wait_ge(w, i * 6 + 2)
                v.tensor_tensor(k2[:], k2[:], bc(m12[:, 3, :].unsqueeze(2), [128, NT, NE]), ALU.mult).then_inc(w, 1)
                v.wait_ge(w, i * 6 + 3)
                v.tensor_tensor(k1[:], k1[:], k2[:], ALU.add).then_inc(w, 1)
                v.wait_ge(w, i * 6 + 4)
                v.tensor_tensor(cw[:, i], k1[:], bc(m12[:, 1, :].unsqueeze(2), [128, NT, NE]), ALU.mult).then_inc(w, 1)
                v.tensor_tensor(lg[:], k1[:], bc(m12[:, 1, :].unsqueeze(2), [128, NT, NE]), ALU.mult).then_inc(w, 1)

            def b2_add(i):
                for t in range(NT):
                    v.wait_ge(S["b2_ps"], i * NT + t + 1)
                    v.tensor_tensor(yt[:, t % 2, :], R[(t + 1) % 2][:, 0:C], gat[:, 1, :], ALU.mult).then_inc(S["b2g"], 1)
                    v.wait_ge(S["b2g"], i * NT + t + 1)
                    v.tensor_tensor(X2[:, i, t, :], X2[:, i, t, :], yt[:, t % 2, :], ALU.add).then_inc(S["x2_2"], 1)

            def sequence(i, first=False, second=False, last=False):
                for h in range(NH):
                    if h == 4 and not (first or second):
                        b2_add(i - 2)
                    maxima(i, h)
                    if h % 4 == 3:
                        max_parts(i, h // 4)
                    if h in (12, 14):
                        o_out(i, (h - 12) // 2)
                    if h % 2 == 0 and h <= 10 and not first:
                        o_out(i - 1, h // 2 + 2)
                    if h == 2 and not (first or second):
                        top2(i - 2)
                        weights(i - 2)
                    if h == 9:
                        v_out(i)
                    if h == 10 and not last:
                        xrot(i + 1)
                        norm_front(i + 1)
                    if h == 11 and not last:
                        h_lo(i + 1)
                    if h == 12 and not last:
                        qk_parts(i + 1)
                    if h == 13 and not first:
                        x2_attn(i - 1)
                    if h == 14 and not first:
                        norm_tail(i - 1)
                    if h == 15 and not first:
                        n_lo(i - 1)

            xrot(0)
            norm_front(0)
            h_lo(0)
            qk_parts(0)
            sequence(0, first=True)
            sequence(1, second=True)
            with v.Fori(2, NB - 1) as i:
                sequence(i)
            sequence(NB - 1, last=True)
            for p in range(2, 8):
                o_out(NB - 1, p)
                if p == 3:
                    top2(NB - 2)
                    weights(NB - 2)
                    b2_add(NB - 2)
            x2_attn(NB - 1)
            norm_tail(NB - 1)
            n_lo(NB - 1)
            top2(NB - 1)
            weights(NB - 1)
            b2_add(NB - 1)
            v.wait_ge(S["x2_2"], NB * NT)
            v.wait_ge(S["xn_out"], NB * 48)

            def group(e, pair, u, later):
                b, g = pair * 2 + u, pair * 2 + (e * NB + u)
                for t in range(HT):
                    v.wait_ge(S["ghi"], g * HT + (t + 1))
                    if later or t >= 3:
                        v.wait_ge(S["m2_ps"], g * HT + (t - 2))
                    v.tensor_tensor(Gl[:, t % 3, :], GF[:, t % 3, :], Gh[:, t % 3, :].bitcast(F32), ALU.subtract)\
                        .then_inc(S["glo"], 1)
                v.wait_ge(S["m2_ps"], (g + 1) * HT)
                v.wait_ge(ld_gc[u], (e * (NB // 2) + pair + 1) * 16)
                for t in range(NT):
                    if later:
                        v.wait_ge(S["acc"], (g - 1) * NT + (t + 1))
                    v.scalar_tensor_tensor(et[:, t, :], m2_bank(t)[:, 0:C], cw[:, b, t, e:e + 1], gc[:, u, :],
                                           ALU.mult, ALU.mult).then_inc(S["eg"], 1)
                for t in range(NT):
                    v.wait_ge(S["eg"], g * NT + (t + 1))
                    v.tensor_tensor(X2[:, b, t, :], X2[:, b, t, :], et[:, t, :], ALU.add).then_inc(S["acc"], 1)

            for u in range(2):
                group(0, 0, u, u > 0)
            with v.Fori(1, NB // 2) as p:
                for u in range(2):
                    group(0, p, u, True)
            for e in range(1, NE):
                with v.Fori(0, NB // 2) as p:
                    for u in range(2):
                        group(e, p, u, True)

        @block.tensor
        def _(pe):
            mm = pe.matmul

            def side(k):
                if k == 2:
                    pe.wait_ge(S["ld_wad"], 16 * 26)
                    pe.wait_ge(S["s_silu"], 3)
                    for s, sec in enumerate((0, 1, 3, 4)):
                        for c in range(3):
                            rows = 128 if c < 2 else STACK
                            dst = bank[2][0:rows, s * 24 + c * 8:s * 24 + c * 8 + 8]
                            for t in range(NCH):
                                w = wad[:, t, sec * C + c * 128:sec * C + c * 128 + 128] if c < 2 else wad2[:, t, s, :]
                                mm(dst, w, sT[:, t, :], start=(t == 0), stop=False)
                            w = bad[:, sec * C + c * 128:sec * C + c * 128 + 128] if c < 2 else bad2[:, s, :]
                            last = mm(dst, w, ones[0:1, 0:NB], start=False, stop=True)
                    last.then_inc(S["p_mods"], 1)
                if 3 <= k < 3 + NB:
                    b = k - 3
                    for g in range(2):
                        if b == 0:
                            pe.wait_ge(S["mods"], 8)
                        else:
                            pe.wait_ge(S["gates"], 2 * (b - 1) + g + 1)
                        cols = slice((2 + 3 * g) * C, (3 + 3 * g) * C)
                        for t in range(NCH):
                            mm(bank[2 + g][0:1, 0:C], sT[:, t, b:b + 1], wad[:, t, cols], start=(t == 0), stop=False)
                        mm(bank[2 + g][0:1, 0:C], ones[0:1, 0:1], bad[:, cols], start=False, stop=True)\
                            .then_inc(S["p_gates"], 1)
                if 12 <= k < 20:
                    n = k - 12
                    pe.wait_ge(ld_wt[n % 4], 16 * (n // 4 + 1))
                    if n < 2:
                        pe.wait_ge(S["gates"], 16)
                    else:
                        pe.wait_ge(S["vf_ready"], n - 1)
                    for t in range(NCH):
                        last = mm(bank[2 + n % 2][0:NB, :], sT[:, t, :], wts[:, n % 4, t, :], start=(t == 0),
                                  stop=(t == NCH - 1))
                    last.then_inc(S["p_vf"], 1)
                if k == 22:
                    pe.wait_ge(S["expm_pool"], UP_DONE)
                    pe.wait_ge(S["vf_ready"], 8)
                    for b in range(NB):
                        last = pe.transpose(bank[2][0:D, b * D:(b + 1) * D], Ab[:, b, :], ident[0:D, 0:D])
                    last.then_inc(S["expm_ps"], 1)
                    pe.wait_ge(S["expm_dve"], ROWSUM_DONE)
                    pe.transpose(bank[3][0:NB, 0:D], rs[:], ident[0:D, 0:D]).then_inc(S["expm_ps"], 1)
                if k == 24:
                    pe.wait_ge(S["expm_pool"], DIAG_DONE)
                    mm(bank[4][0:D, 0:NB * (NSQ + 1)], ones[0:NB, 0:D], dg[:].rearrange("p b t -> p (b t)"),
                       start=True, stop=True).then_inc(S["expm_ps"], 1)
                if k == 26:
                    pe.wait_ge(S["expm_dve"], SCALED_DONE)
                    products(bank[2], Ab, Ab, S["expm_ps"])
                if k == 27:
                    pe.wait_ge(S["expm_act"], A2_DONE)
                    products(bank[3], A2, Ab, S["expm_ps"])
                    pe.wait_ge(S["expm_act"], FLAGS_SPREAD)
                    products(bank[4], A2, A2, S["expm_ps"])
                if k == 28:
                    pe.wait_ge(S["expm_dve"], B2_DONE)
                    pe.wait_ge(S["expm_act"], A4_DONE)
                    products(bank[2], A4, Bk, S["expm_ps"])
                    pe.wait_ge(S["expm_dve"], H1_DONE)
                    products(bank[3], A4, L, S["expm_ps"])
                if k == 30:
                    pe.wait_ge(S["expm_dve"], R_DONE)
                    for b in range(NB):
                        last = pe.transpose(bank[4][0:D, b * D:(b + 1) * D], RR[:, b, :], ident[0:D, 0:D])
                    last.then_inc(S["expm_ps"], 1)
                if 31 <= k < 31 + 2 * NSQ:
                    t, half = (k - 31) // 2, (k - 31) % 2
                    pe.wait_ge(S["lr_ready"], 2 * t + 2)
                    if half == 0:
                        products(bank[2], LT, RR, S["p_sq"])
                    else:
                        products(bank[3], L, RT, S["p_sq"])

            def products(dst, lhsT, rhs, done):
                for b in range(NB):
                    last = mm(dst[0:D, b * D:(b + 1) * D], lhsT[:, b, :], rhs[:, b, :], start=True, stop=True)
                last.then_inc(done, 1)

            pe.wait_ge(S["const"], 1)
            pe.wait_ge(S["ld_P"], 16)
            for j in range(D):
                if j:
                    pe.wait_ge(S["upd"], 3 * j)
                mm(R[1][0:CH, j:D], bc(ident[0:CH, j:j + 1], [CH, CH]), A[:, 0, j:D], start=True, stop=True)\
                    .then_inc(S["qrE"], 1)
                pe.wait_ge(S["a0"], j + 1)
                for t in (1, 2):
                    mm(R[0][0:CH, j:D], bc(A[:, t, j:j + 1], [CH, CH]), A[:, t, j:D], start=(t == 1), stop=False)
                mm(R[0][0:CH, j:D], bc(a0m[:, j % 2:j % 2 + 1], [CH, CH]), A[:, 0, j:D], start=False, stop=True)\
                    .then_inc(S["qrD"], 1)
                side(j)
            pe.wait_ge(S["V_ready"], 1)
            pe.wait_ge(S["sq_ready"], 2 * NSQ)
            for t in range(NCH):
                last = mm(R[0][0:D, 0:D], A[:, t, :], A[:, t, :], start=(t == 0), stop=(t == NCH - 1))
            last.then_inc(S["expm_ps"], 1)
            for t in range(NCH):
                last = pe.transpose(bank[2][0:D, t * CH:(t + 1) * CH], A[:, t, :], ident[0:CH, 0:CH])
            last.then_inc(S["expm_ps"], 1)
            pe.wait_ge(S["expm_dve"], X_DONE)
            pe.transpose(bank[3][0:D, 0:D], XX[:, 0, :], ident[0:D, 0:D]).then_inc(S["expm_ps"], 1)
            for k in range(6):
                pe.wait_ge(S["XT_ready"], k + 1)
                pe.wait_ge(S["Y_ready"], k + 1)
                mm(bank[5][0:D, 0:D], XX[:, 1, :], Y[:], start=True, stop=True).then_inc(S["p_Y"], 1)
                if k < 5:
                    mm(bank[4][0:D, 0:D], XX[:, 1, :], XX[:, 0, :], start=True, stop=True)
                    mm(bank[4][0:D, D:2 * D], XX[:, 0, :], XX[:, 1, :], start=True, stop=True).then_inc(S["p_X"], 1)
            pe.wait_ge(S["Y_ready"], 7)
            for t in range(NCH):
                last = mm(bank[6][0:CH, t * D:(t + 1) * D], VT[:, t * CH:(t + 1) * CH], Y[:], start=True, stop=True)
            last.then_inc(S["p_U"], 1)
            mm(bank[7][0:D, 0:C], Y[:], VT[:], start=True, stop=True).then_inc(S["p_U"], 1)
            pe.wait_ge(S["U_ready"], 4)
            pe.wait_ge(S["rotm"], 1)
            for b in range(NB):
                mm(bank[b][0:D, 0:C], RT[:, b, :], UT[:], start=True, stop=True).then_inc(S["p_rot"], 1)
            pe.wait_ge(S["rot_ready"], NB)
            pe.wait_ge(S["wq_split"], 5)
            pe.wait_ge(S["ld_misc"], 16 * (4 + MT))

            read = [None, None]

            def ring(k, done, value):
                if read[k % 2] is not None:
                    pe.wait_ge(*read[k % 2])
                read[k % 2] = (done, value)
                return R[k % 2]

            def transposed(i, src, width, ps, readers):
                for c in range(3):
                    rows = min(width, (XW if width == 128 else C) - c * width)
                    r = ring(c, readers, i * 3 + c + 1)
                    for t in range(NT):
                        last = pe.transpose(r[0:rows, t * 128:(t + 1) * 128], src[:, t, c * width:c * width + rows], ident[:])
                    last.then_inc(ps, 1)

            def split_mm(dst, left, right, n):
                (lh, ll), (rh, rl) = left, right
                k = 0
                for c in range(2):
                    for p, q in ((lh, rh), (ll, rh), (lh, rl)):
                        mm(dst, p(c), q(c), start=(k == 0), stop=False)
                        k += 1
                return mm(dst, lh(2), rh(2), start=False, stop=True)

            def f_xT(i):
                pe.wait_ge(S["ld_x"], i * 16 + 16)
                transposed(i, xin, CH, S["xT_ps"], S["xT_sb"])

            def f_z(i):
                pe.wait_ge(S["xT_sb"], i * 3 + 3)
                r = ring(1, S["z_sb"], i + 1)
                for c in range(NCH):
                    last = mm(r[0:D, :], U[:, c, :], xT[:, c, :], start=(c == 0), stop=(c == NCH - 1))
                last.then_inc(S["z_ps"], 1)

            def f_delta(i):
                pe.wait_ge(S["z_sb"], i + 1)
                pe.wait_ge(S["ld_rot"], i * 16 + 16)
                for t in range(NT):
                    r = ring(t, S["xrot"], i * NT + t + 1)
                    mm(r[:, 0:C], zT[:, t * 128:(t + 1) * 128], rot[:], start=True, stop=True).then_inc(S["delta_ps"], 1)

            def f_hT(i):
                pe.wait_ge(S["xh_f1"], i * 8 + 8)
                transposed(i, xh, 128, S["hT_ps"], S["hF"])

            def f_qk(i):
                pe.wait_ge(S["hHi"], i * 4 + 4)
                pe.wait_ge(S["hLo"], i * 2 + 2)
                for m in range(MT):
                    rows = MROWS[m]
                    cols = slice(m * HP * HD, m * HP * HD + rows)
                    r = ring(m + 1, S["qkh"], i * MT + m + 1)
                    split_mm(r[0:rows, :],
                             (lambda c: wqh[0:128 if c < 2 else STACK, c, cols], lambda c: wql[:, c, cols]),
                             (lambda c: Hh[0:128 if c < 2 else STACK, c, :], lambda c: Hl[:, c, :]), 512)\
                        .then_inc(S["qk_ps"], 1)

            def m_v(i):
                for t in range(NT):
                    tok = slice(t * 128, (t + 1) * 128)
                    r = ring(t, S["v_sb"], i * NT + t + 1)
                    split_mm(r[:, 0:C],
                             (lambda c: Hh[0:128 if c < 2 else STACK, c, tok], lambda c: Hl[:, c, tok]),
                             (lambda c: wqh[0:128 if c < 2 else STACK, c, 2 * C:3 * C], lambda c: wql[:, c, 2 * C:3 * C]), C)\
                        .then_inc(S["v_ps"], 1)

            def m_scores(i, h, t):
                r = ring(t, S["smax"], i * 64 + (4 * h + t + 1))
                mm(r[:], Qs[0:KROWS, h, t * 128:(t + 1) * 128], Ks[0:KROWS, h, :], start=True, stop=True)\
                    .then_inc(S["s_ps"], 1)

            def m_shifted(i, h, k):
                if h % 4 == 0 and k == 0:
                    pe.wait_ge(m_in[h // 4 % 2], (i * 2 + (h // 8 + 1)) * 16)
                if h or not fixed(i, 0):
                    pe.wait_ge(S["expd"], i * 32 + (2 * h - 1 + k))
                for n in range(2):
                    kt = 2 * k + n
                    last = mm(ST[k][:, n, :], Ks[0:KROWS + NPART, h, kt * 128:(kt + 1) * 128], Qs[0:KROWS + NPART, h, :],
                              start=True, stop=True)
                last.then_inc(S["st_ps"], 1)

            def m_av(i, h, k):
                if h == 0 and k == 0:
                    pe.wait_ge(S["v_sb"], i * NT + NT)
                if k == 0 and (h or not fixed(i, 0)):
                    pe.wait_ge(S["avT"], i * NH + h)
                pe.wait_ge(S["expd"], i * 32 + (2 * h + k + 1))
                for kt in (2 * k, 2 * k + 1):
                    last = mm(OB[0][0:VW, :], Va[:, kt, h, :], PT[:, h % 2, kt, :], start=(kt == 0), stop=(kt == NT - 1))
                last.then_inc(S["av_ps"], 1)

            def m_tok(i, h):
                p = h // 2
                if h % 2 == 0 and (p or not fixed(i, 0)):
                    pe.wait_ge(S["o_sb"], i * 8 + p)
                wait_apart(pe, S["avT"], i * NH + (h + 1))
                for t in range(NT):
                    last = pe.transpose(tok[:, t, h % 2, :], oTh[:, t * 128:(t + 1) * 128], ident[0:VW, 0:VW])
                last.then_inc(S["tok_ps"], 1)

            def m_mT(i, q):
                pe.wait_ge(S["mparts"], i * 16 + 4 * q + 4)
                r = ring(0, S["mT_sb"], i * 4 + q + 1)
                pe.sem_inc(S["apart"], 1)
                pe.transpose(r[0:48, 0:64].bitcast(BF16), mp[:].rearrange("p k n -> p (k n)"), identb[:])\
                    .then_inc(S["mT_ps"], 1)

            def t_oT(i):
                pe.wait_ge(S["o_sb"], i * 8 + 8)
                transposed(i, o, CH, S["oT_ps"], S["oT_sb"])

            def t_proj(i):
                pe.wait_ge(S["oT_sb"], i * 3 + 3)
                for t in range(NT):
                    r = ring(t, S["yg"], i * 8 + 2 * t + 1)
                    for c in range(NCH):
                        last = mm(r[:, 0:C], xT[:, c, t * 128:(t + 1) * 128], wp[:, c, :], start=(c == 0), stop=(c == NCH - 1))
                    last.then_inc(S["proj_ps"], 1)

            def t_nT(i):
                pe.wait_ge(S["xh_n"], i * 8 + 8)
                transposed(i, xh, 128, S["nT_ps"], S["nF"])

            def t_gate(i):
                pe.wait_ge(S["nHi"], i * 4 + 4)
                pe.wait_ge(S["nLo"], i * 2 + 2)
                r = ring(0, S["lgc"], i * 20 + 1)
                for t in range(NT):
                    tok = slice(t * 128, (t + 1) * 128)
                    last = split_mm(r[:, t * NE:(t + 1) * NE],
                                    (lambda c: Nh[0:128 if c < 2 else STACK, c, tok], lambda c: Nl[:, c, tok]),
                                    (lambda c: wgh[0:128 if c < 2 else STACK, c, :], lambda c: wgl[:, c, :]), NE)
                last.then_inc(S["gl_ps"], 1)

            def t_cwT(i):
                pe.wait_ge(S["cw_ready"], i * 6 + 6)
                r = ring(0, S["cwT_sb"], i + 1)
                for t in range(NT):
                    last = pe.transpose(r[0:NE, t * 128:(t + 1) * 128], lg[:, t, :], ident[:])
                last.then_inc(S["cwT_ps"], 1)

            def t_b2(i):
                pe.wait_ge(S["cwT_sb"], i + 1)
                for t in range(NT):
                    r = ring(t + 1, S["b2g"], i * NT + t + 1)
                    mm(r[:, 0:C], zT[0:NE, t * 128:(t + 1) * 128], b2s[:], start=True, stop=True).then_inc(S["b2_ps"], 1)

            def sequence(i, first=False, second=False, last=False):
                for h in range(NH):
                    def behind(n):
                        return (i, h - n) if h >= n else None if first else (i - 1, h - n + NH)
                    st, av, tk = behind(8), behind(10), behind(11)
                    if h % 4 == 0:
                        pe.wait_ge(qin[h // 4], (i + 1) * 144)
                    if h == 4 and not (first or second):
                        t_cwT(i - 2)
                        t_b2(i - 2)
                    m_scores(i, h, 0)
                    m_scores(i, h, 1)
                    if tk:
                        m_tok(*tk)
                    if av:
                        m_av(*av, 0)
                    if st:
                        m_shifted(*st, 0)
                    m_scores(i, h, 2)
                    if av:
                        m_av(*av, 1)
                    m_scores(i, h, 3)
                    if st:
                        m_shifted(*st, 1)
                    if h == 2 and not (first or second):
                        t_gate(i - 2)
                    if h == 8 and not last:
                        f_xT(i + 1)
                    if h == 9:
                        m_v(i)
                        if not last:
                            f_z(i + 1)
                    if h == 10 and not last:
                        f_delta(i + 1)
                    if h == 11:
                        if not last:
                            f_hT(i + 1)
                        if not first:
                            t_oT(i - 1)
                    if h == 12 and not last:
                        f_qk(i + 1)
                    if h == 13 and not first:
                        t_proj(i - 1)
                    if h == 15 and not first:
                        t_nT(i - 1)
                    if h % 4 == 3:
                        m_mT(i, h // 4)

            f_xT(0)
            f_z(0)
            f_delta(0)
            f_hT(0)
            f_qk(0)
            pe.wait_ge(S["kones"], 1)
            sequence(0, first=True)
            sequence(1, second=True)
            with pe.Fori(2, NB - 1) as i:
                read[:] = [(S["mT_sb"], i * 4), (S["smax"], i * 64)]
                sequence(i)
            read[:] = [(S["mT_sb"], (NB - 1) * 4), (S["smax"], (NB - 1) * 64)]
            sequence(NB - 1, last=True)
            for h in range(8, NH + 3):
                if h == 12:
                    t_cwT(NB - 2)
                    t_b2(NB - 2)
                if h - 3 < NH:
                    m_tok(NB - 1, h - 3)
                if h - 2 < NH:
                    m_av(NB - 1, h - 2, 0)
                if h < NH:
                    m_shifted(NB - 1, h, 0)
                if h - 2 < NH:
                    m_av(NB - 1, h - 2, 1)
                if h < NH:
                    m_shifted(NB - 1, h, 1)
                if h == 10:
                    t_gate(NB - 2)
            t_oT(NB - 1)
            t_proj(NB - 1)
            t_nT(NB - 1)
            t_gate(NB - 1)
            t_cwT(NB - 1)
            t_b2(NB - 1)
            pe.wait_ge(S["x2_2"], NB * NT)

            def group(e, pair, u, later):
                g = e * NB + (pair * 2 + u)
                pe.wait_ge(ld_xn[u], (e * (NB // 2) + pair + 1) * 32)

                def hidden(t):
                    pe.wait_ge(S["w_lo"], e * (3 * HT) + 3 * (t + 1))
                    if later or t >= 3:
                        pe.wait_ge(S["gelu"], g * HT + (t - 2))
                    split_mm(m1_bank(t),
                             (lambda c: w1h[0:128 if c < 2 else STACK, t, c, :], lambda c: w1l[:, t, c, :]),
                             (lambda c: xn[:, u, c, :] if c < 2 else xn[0:STACK, u, 4, :], lambda c: xn[:, u, 2 + c, :]), 512)\
                        .then_inc(S["m1_ps"], 1)

                def combine(t):
                    pe.wait_ge(S["glo"], g * HT + (t + 1))
                    if t == 0 and later:
                        pe.wait_ge(S["eg"], g * NT)
                    for m in range(NT):
                        tok = slice(m * 128, (m + 1) * 128)
                        dst = m2_bank(m)[:, 0:C]
                        mm(dst, Gh[:, t % 3, tok], w2h[:, t, :], start=(t == 0), stop=False)
                        mm(dst, Gh[:, t % 3, tok], w2l[:, t, :], start=False, stop=False)
                        last = mm(dst, Gl[:, t % 3, tok], w2h[:, t, :], start=False, stop=(t == HT - 1))
                    last.then_inc(S["m2_ps"], 1)

                for t in range(HT + 2):
                    if t < HT:
                        hidden(t)
                    if t >= 2:
                        combine(t - 2)

            for u in range(2):
                group(0, 0, u, u > 0)
            with pe.Fori(1, NB // 2) as p:
                for u in range(2):
                    group(0, p, u, True)
            with pe.Fori(1, NE) as e:
                with pe.Fori(0, NB // 2) as p:
                    for u in range(2):
                        group(e, p, u, True)


def kernel(**inputs):
    import numpy as _np
    import concourse.bacc as _bacc
    from concourse.bass_utils import run_bass_kernel_spmd as _run

    get = lambda k: _np.ascontiguousarray(inputs[k])
    W = get("L0_cond_W")
    iu, ju = _np.triu_indices(D, k=1)
    WT = _np.zeros((C, D * D), W.dtype)
    WT[:, iu * D + ju] = W.T
    bU = _np.zeros((D, D), W.dtype)
    bU[iu, ju] = get("L0_cond_b")
    arrays = {
        "x": get("x"), "condT": _np.ascontiguousarray(get("cond_1152").T), "P": get("L0_cond_P"), "WT": WT, "bU": bU,
        "w_adaln": get("L1_cond_w_adaln"), "b_adaln": get("L1_cond_b_adaln"), "w_qkv": get("L1_cond_w_qkv"),
        "b_qkv": get("L1_cond_b_qkv"), "w_proj": get("L1_cond_w_proj"), "b_proj": get("L1_cond_b_proj"),
        "w_gate": get("L1_cond_w_gate"), "w1": get("L1_cond_w1"), "b1T": _np.ascontiguousarray(get("L1_cond_b1").reshape(NE * HT, 128).T), "w2": get("L1_cond_w2"),
        "b2": get("L1_cond_b2"),
    }
    nc = _bacc.Bacc("TRN2", target_bir_lowering=False, num_devices=1)
    args = [nc.dram_tensor(f"in_{k}", a.shape, F32, kind="ExternalInput").ap() for k, a in arrays.items()]
    y = nc.dram_tensor("out_y", (NB, T, C), F32, kind="ExternalOutput").ap()
    build(nc, *args, y)
    r = _run(nc, [{f"in_{k}": a for k, a in arrays.items()}], core_ids=[0])
    return r.results[0]["out_y"]
```

```python
from contextlib import ExitStack

import concourse.bass as bass
from concourse import mybir

F32 = mybir.dt.float32
F32R = mybir.dt.float32r
BF16 = mybir.dt.bfloat16
ALU = mybir.AluOpType
ACT = mybir.ActivationFunctionType
AX = mybir.AxisListType

NB, T, C = 8, 512, 288
NT = T // 128
D = 64
CH = 96
NCH = C // CH
NH = 16
HD = C // NH
HP = 7
MT = 5
MROWS = [HP * HD] * 4 + [2 * C - 4 * HP * HD]
NPAIR = 6
KROWS = NPAIR * HD
NPART = 3
SCALE = HD ** -0.5
NE = 4
HID = 1152
HT = HID // 128
STACK = 96
XW = 256 + STACK
VW = 20
NSQ = 16

PS_UPT, PS_RST, PS_FS, PS_A2, PS_A3, PS_A4, PS_H1, PS_H2, PS_RT, PS_S, PS_VT, PS_XT = range(1, 13)
FLAGS_SPREAD, A2_DONE, A3_DONE, A4_DONE, RT_DONE, VT_DONE = range(1, 7)
SKEW_DONE, ROWSUM_DONE, FLAGS_DONE, SCALED_DONE, B2_DONE, H1_DONE, R_DONE, X_DONE = range(1, 9)
UP_DONE, DIAG_DONE = range(1, 3)

def vf_step(piece):
    return 3 + piece * 2 // 3


MODS_AT = tuple(range(19, 31))
GATES_AT = (60, 62)
SQ0 = 31

TAYLOR = [1.0]
for _k in range(1, 12):
    TAYLOR.append(TAYLOR[-1] / _k)


def build(nc, x, condT, P, WT, bU, w_adaln, b_adaln, w_qkv, b_qkv, w_proj, b_proj, w_gate, w1, b1T, w2, b2, out):
    up_d = nc.dram_tensor("up_scratch", (NB, D, D), F32).ap()
    gate_d = nc.dram_tensor("gate_scratch", (NB, 2, C), F32).ap()
    rot_d = nc.dram_tensor("rot_scratch", (NB, D, C), F32).ap()
    mod_d = nc.dram_tensor("mod_scratch", (NB, 128, 12), F32).ap()
    qk_d = nc.dram_tensor("qk_scratch", (2 * NH, NPART, HD, T), BF16).ap()
    xn_d = nc.dram_tensor("xn_scratch", (NB, 128, 5, T), F32).ap()

    with ExitStack() as ctx:
        def sb(name, shape, dt=F32, c=ctx):
            return c.enter_context(nc.sbuf_tensor(name, shape, dt))

        def sem(name):
            return ctx.enter_context(nc.semaphore(name))

        R = [ctx.enter_context(nc.psum_tensor(f"ringR{k}", [128, 512], F32)) for k in range(2)]
        ST = [ctx.enter_context(nc.psum_tensor(f"ringS{k}", [128, 2, 512], F32)) for k in range(2)]
        OB = [ctx.enter_context(nc.psum_tensor(f"bankO{k}", [128, 512], F32)) for k in range(2)]
        bank = [R[0][:], R[1][:], ST[0][:, 0], ST[0][:, 1], ST[1][:, 0], ST[1][:, 1], OB[0][:], OB[1][:]]

        ident = sb("ident", [128, 128])
        identb = sb("identb", [128, 128], BF16)
        ones = sb("ones", [128, 128])
        nhalf = sb("nhalf", [128, 4])
        X2 = sb("X2", [128, NB, NT, C])
        cw = sb("cw", [128, NB, NT, NE])

        ab = ctx.enter_context(ExitStack())
        wp = sb("wp", [CH, NCH, C], F32, ab)
        wgh = sb("wgh", [128, 3, NE], F32R, ab)
        wgl = sb("wgl", [128, 2, NE], F32R, ab)
        b2s = sb("b2s", [NE, C], F32, ab)
        bp = sb("bp", [128, C], F32, ab)
        xT = sb("xT", [CH, NCH, T], F32, ab)
        zT = sb("zT", [D, T], F32, ab)
        wqh = sb("wqh", [128, 3, 3 * C], F32R, ab)
        wql = sb("wql", [128, 2, 3 * C], F32R, ab)
        bqk = sb("bqk", [128, MT], F32, ab)
        bv = sb("bv", [128, C], F32, ab)
        U = sb("U", [CH, NCH, D], F32, ab)
        xin = sb("xin", [128, NT, C], F32, ab)

        a = ctx.enter_context(ExitStack())
        wqr = sb("wqr", [128, 3, 3 * C], F32, a)
        wgr = sb("wgr", [128, 3, NE], F32, a)
        A = sb("A", [CH, NCH, D], F32, a)
        V0 = sb("V0", [CH, D], F32, a)
        a0m = sb("a0m", [CH, 2], F32, a)
        maskge = sb("maskge", [CH, D], F32, a)
        striu = sb("striu", [D, D], F32, a)
        Es = sb("Es", [CH, D], F32, a)
        sc = sb("sc", [CH, 16], F32, a)
        t1 = sb("t1", [CH, D], F32, a)
        cc = sb("cc", [CH, D], F32, a)
        VT = sb("VT", [D, C], F32, a)
        XX = sb("XX", [D, 2, D], F32, a)
        Y = sb("Y", [D, D], F32, a)
        UT = sb("UT", [D, C], F32, a)
        dd = sb("dd", [D, 4], F32, a)
        sT = sb("sT", [CH, NCH, NB], F32, a)
        cT = sb("cT", [CH, NCH, NB], F32, a)
        eT = sb("eT", [CH, NCH, NB], F32, a)
        wad = sb("wad", [CH, NCH, 6 * C], F32, a)
        wad2 = sb("wad2", [CH, NCH, 4, STACK], F32, a)
        bad = sb("bad", [1, 6 * C], F32, a)
        bad2 = sb("bad2", [1, 4, STACK], F32, a)
        modt = sb("modt", [128, NB, 12], F32, a)
        gts = sb("gts", [NB, 2, C], F32, a)
        wts = sb("wts", [CH, 4, NCH, 512], F32, a)
        vf = sb("vf", [NB, D * D], F32, a)
        bUs = sb("bUs", [D, D], F32, a)
        Ab = sb("Ab", [D, NB, D], F32, a)
        A2 = sb("A2", [D, NB, D], F32, a)
        A3 = sb("A3", [D, NB, D], F32, a)
        A4 = sb("A4", [D, NB, D], F32, a)
        Bk = sb("Bk", [D, NB, D], F32, a)
        RR = sb("RR", [D, NB, D], F32, a)
        RT = sb("RT", [D, NB, D], F32, a)
        L = sb("L", [D, NB, D], F32, a)
        rs = sb("rs", [D, NB], F32, a)
        nrm = sb("nrm", [NB, 2], F32, a)
        pw = sb("pw", [NB, 2, NSQ], F32, a)
        fs = sb("fs", [NB, NSQ + 1], F32, a)
        fq = sb("fq", [NB, NSQ], F32, a)
        dg = sb("dg", [NB, NB, NSQ + 1], F32, a)
        fsb = sb("fsb", [D, NB, NSQ + 1], F32, a)
        Gs = sb("Gs", [D, NB, C], F32, a)
        a.close()

        Qs = sb("Qs", [128, NH, T], BF16, ab)
        Ks = sb("Ks", [128, NH, T], BF16, ab)
        PT = sb("PT", [128, 2, NT, T], F32, ab)
        Va = sb("Va", [128, NT, NH, VW], F32, ab)
        oTh = sb("oTh", [VW, T], F32, ab)
        st6 = sb("st6", [128, 2, NT, 6], F32, ab)
        mv = sb("mv", [128, 2, NT, 2], F32, ab)
        ve = sb("ve", [128, 2, NT], F32, ab)
        rstd = sb("rstd", [128, 2, NT], F32, ab)
        xh = sb("xh", [128, NT, XW], F32, ab)
        F = sb("F", [128, 3, T], F32, ab)
        prt = sb("prt", [128, 2, NPART, T], BF16, ab)
        Hh = sb("Hh", [128, 3, T], F32R, ab)
        Hl = sb("Hl", [128, 2, T], F32R, ab)
        Nh = sb("Nh", [128, 3, T], F32R, ab)
        Nl = sb("Nl", [128, 2, T], F32R, ab)
        QF = sb("QF", [128, 2, T], F32, ab)
        mx = sb("mx", [128, NT, NH // NT, NT], F32, ab)
        mr = sb("mr", [128, 16], F32, ab)
        mp = sb("mp", [128, NPART, 16], BF16, ab)
        mTs = sb("mTs", [48, 2, 128], BF16, ab)
        rec = sb("rec", [128, 2, NT, 2], F32, ab)
        o = sb("o", [128, NT, C], F32, ab)
        gat = sb("gat", [128, 2, C], F32, ab)
        rot = sb("rot", [D, C], F32, ab)
        modf = sb("modf", [128, 12], F32, ab)
        modn = sb("modn", [128, 12], F32, ab)
        yt = sb("yt", [128, 2, C], F32, ab)
        lg = sb("lg", [128, NT, NE], F32, ab)
        k1 = sb("k1", [128, NT, NE], F32, ab)
        k2 = sb("k2", [128, NT, NE], F32, ab)
        us = sb("us", [128, NT, NE], F32, ab)
        l2 = sb("l2", [128, NT, NE], F32, ab)
        m12 = sb("m12", [128, 4, NT], F32, ab)
        ab.close()

        GF = sb("GF", [128, 3, T])
        et = sb("et", [128, 4, C])
        b1s = sb("b1s", [128, NE * HT])
        gc = sb("gc", [128, 2, C])
        wr = sb("wr", [128, HT, 3, 128], F32)
        vr = sb("vr", [128, HT, C], F32)
        w1h = sb("w1h", [128, HT, 3, 128], F32R)
        w1l = sb("w1l", [128, HT, 2, 128], F32R)
        w2h = sb("w2h", [128, HT, C], F32R)
        w2l = sb("w2l", [128, HT, C], F32R)
        xn = sb("xn", [128, 2, 5, T], F32R)
        Gh = sb("Gh", [128, 3, T], F32R)
        Gl = sb("Gl", [128, 3, T], F32R)

        names = """const ld_P ld_cond ld_wad ld_misc ld_wq ld_bU
 e_silu s_silu p_mods mods p_gates gates mod_out gate_out p_vf vf_ready vf_out up_in expm_pool expm_ps expm_dve expm_act
 p_sq sq_ready rotm p_rot rot_ready rot_out
 qrE qrD sigma upd a0 V_ready XT_ready p_Y Y_ready p_X p_U U_ready 
 wq_split dch pch
 kones vones ld_x ld_rot ld_modf ld_modn ld_gat
 xT_ps xT_sb z_ps z_sb delta_ps xrot bst mvf var_eps rstd_f xh_f1 hT_ps hF hHi hLo
 qk_ps qkF qkh qkr qkm qkl v_ps v_sb s_ps smax mparts mT_ps mT_sb st_ps expd av_ps avT tok_ps orec o_sb oT_ps oT_sb proj_ps yg x2_1
 bst2 mvn var_eps2 rstd_n xh_n nT_ps nF nHi nLo xn_out
 gl_ps lgc top g_exp cw_ready cwT_ps cwT_sb b2_ps b2g x2_2
 ld_b1 w_free w_hi w_lo m1_ps gelu ghi glo m2_ps eg acc apart""".split()
        S = {n: sem(n) for n in names}
        qin = [sem(f"qk_in_quad{k}") for k in range(4)]
        wraw = [sem(f"w_raw{t}") for t in range(HT)]
        ld_wt = [sem(f"ld_wt{k}") for k in range(4)]
        parts_out = [sem(f"parts_out{k}") for k in range(2)]
        m_in = [sem(f"max_in{k}") for k in range(2)]
        ld_xn = [sem(f"ld_xn{k}") for k in range(2)]
        ld_gc = [sem(f"ld_gc{k}") for k in range(2)]
        yout = sem("y_stored")

        block = ctx.enter_context(nc.Block())

        def fixed(i, n):
            return isinstance(i, int) and i == n

        def parts_stored(i, m):
            return (i * (3 - m % 2) + (m // 2 + 1)) * NPART * 16

        tok = OB[1][:, 0:NT * 2 * VW].rearrange("p (t s d) -> p t s d", t=NT, s=2)

        def m1_bank(t):
            return (ST[0][:, 0, :], ST[0][:, 1, :], ST[1][:, 0, :])[t % 3]

        def m2_bank(t):
            return (R[0][:], R[1][:], OB[0][:], OB[1][:])[t]

        def behind(i, h, n, first):
            return (i, h - n) if h >= n else None if first else (i - 1, h - n + NH)

        def quad_before(i, h):
            return (i, h // 4 - 1) if h else (i - 1, 3)

        XT_AT, Z_AT, DELTA_AT, NORM_AT, HT_AT, HLO_AT = 1, 3, 5, 6, 7, 10
        QK_AT = {11: (0, 1), 12: (2,), 13: (3, 4)}
        V_AT = 9
        OT_AT, NORM2_AT = 11, 15
        PROJ_AT = {12: (0, 1), 14: (2, 3)}
        NT_AT, GATE_AT, CW_AT, B2_AT = 2, 4, 7, 8

        def wait_apart(engine, sem, value):
            engine.wait_ge(sem, value)
            engine.sem_inc(S["apart"], 1)

        def bc(ap, shape):
            return ap.to_broadcast(shape)

        @block.sync
        def _(sp):
            sp.dma_start(A[:], P.rearrange("(t p) d -> p t d", p=CH)).then_inc(S["ld_P"], 16)
            sp.dma_start(cT[:], condT.rearrange("(t p) b -> p t b", p=CH)).then_inc(S["ld_cond"], 16)

            def load_wt(n):
                sp.dma_start(wts[:, n % 4], WT[:, n * 512:(n + 1) * 512].rearrange("(t p) n -> p t n", p=CH))\
                    .then_inc(ld_wt[n % 4], 16)

            for n in range(4):
                load_wt(n)
            sp.dma_start(bUs[:], bU).then_inc(S["ld_bU"], 16)
            sp.dma_start(xin[:], x[0].rearrange("(t p) c -> p t c", p=128)).then_inc(S["ld_x"], 16)
            for n in range(4, 8):
                sp.wait_ge(S["p_vf"], n - 3)
                load_wt(n)
            sp.dma_start(wad[:], w_adaln.rearrange("(t p) n -> p t n", p=CH)).then_inc(S["ld_wad"], 16)
            sp.dma_start(bad[:], b_adaln.rearrange("(o n) -> o n", o=1)).then_inc(S["ld_wad"], 16)
            for k, s in enumerate((0, 1, 3, 4)):
                for r in range(3):
                    sp.dma_start(wad2[:, :, k, 32 * r:32 * r + 32],
                                 w_adaln[:, s * C + 256:(s + 1) * C].rearrange("(t p) n -> p t n", p=CH)).then_inc(S["ld_wad"], 16)
                    sp.dma_start(bad2[:, k, 32 * r:32 * r + 32],
                                 b_adaln[s * C + 256:(s + 1) * C].rearrange("(o n) -> o n", o=1)).then_inc(S["ld_wad"], 16)
            sp.wait_ge(S["vf_ready"], 8)
            sp.dma_start(up_d.rearrange("b i j -> b (i j)"), vf[:]).then_inc(S["vf_out"], 16)
            sp.wait_ge(S["vf_out"], 16)
            sp.dma_start(Ab[:], up_d.rearrange("b i j -> i b j")).then_inc(S["up_in"], 16)
            sp.dma_start(wqr[:, 0:2, :], w_qkv[0:256, :].rearrange("(t p) n -> p t n", p=128)).then_inc(S["ld_wq"], 16)
            sp.dma_start(wgr[:, 0:2, :], w_gate[0:256, :].rearrange("(t p) n -> p t n", p=128)).then_inc(S["ld_wq"], 16)
            for r in range(3):
                sp.dma_start(wqr[32 * r:32 * r + 32, 2, :], w_qkv[256:C, :]).then_inc(S["ld_wq"], 16)
                sp.dma_start(wgr[32 * r:32 * r + 32, 2, :], w_gate[256:C, :]).then_inc(S["ld_wq"], 16)
            sp.dma_start(wp[:], w_proj.rearrange("(t p) n -> p t n", p=CH)).then_inc(S["ld_misc"], 16)
            sp.dma_start(b2s[:], b2).then_inc(S["ld_misc"], 16)
            for m in range(MT):
                sp.dma_start(bqk[0:MROWS[m], m:m + 1],
                             b_qkv[m * HP * HD:m * HP * HD + MROWS[m]].rearrange("(p o) -> p o", o=1)).then_inc(S["ld_misc"], 16)
            sp.dma_start(bv[:], b_qkv[2 * C:3 * C].partition_broadcast(128)).then_inc(S["ld_misc"], 16)
            sp.dma_start(bp[:], b_proj.partition_broadcast(128)).then_inc(S["ld_misc"], 16)
            sp.wait_ge(S["mods"], 8)
            sp.dma_start(mod_d.rearrange("b p k -> p b k"), modt[:]).then_inc(S["mod_out"], 16)
            sp.wait_ge(S["gates"], 2)
            sp.dma_start(gate_d, gts[:]).then_inc(S["gate_out"], 16)
            sp.wait_ge(S["rot_ready"], 8)
            sp.dma_start(rot_d.rearrange("b d n -> d b n"), Gs[:]).then_inc(S["rot_out"], 16)
            sp.wait_ge(S["rot_out"], 16)
            sp.wait_ge(S["mod_out"], 16)
            sp.wait_ge(S["gate_out"], 16)
            sp.wait_ge(S["wq_split"], 5)

            def load_front(i):
                if not (isinstance(i, int) and i == 0):
                    wait_apart(sp, S["xrot"], i * NT)
                    sp.wait_ge(S["xT_ps"], i * 3)
                    sp.wait_ge(S["delta_ps"], i * NT)
                    wait_apart(sp, S["hF"], i * 3)
                    sp.dma_start(xin[:], x[i].rearrange("(t p) c -> p t c", p=128)).then_inc(S["ld_x"], 16)
                sp.dma_start(rot[:], rot_d[i]).then_inc(S["ld_rot"], 16)
                sp.dma_start(modf[:], mod_d[i]).then_inc(S["ld_modf"], 16)

            def load_tail(i):
                if not (isinstance(i, int) and i == 0):
                    wait_apart(sp, S["nF"], i * 3)
                    wait_apart(sp, S["b2g"], i * NT)
                sp.dma_start(modn[:], mod_d[i]).then_inc(S["ld_modn"], 16)
                sp.dma_start(gat[:], gate_d[i].partition_broadcast(128)).then_inc(S["ld_gat"], 16)

            def store_parts(i, tiles=range(MT)):
                if 0 in tiles and not fixed(i, 0):
                    for q in range(4):
                        wait_apart(sp, qin[q], i * 144)
                for m in tiles:
                    wait_apart(sp, S["qkl"], i * MT + m + 1)
                    n = MROWS[m] // HD
                    for p in range(NPART):
                        sp.dma_start(qk_d[m * HP:m * HP + n, p], prt[0:MROWS[m], m % 2, p, :]).then_inc(parts_out[m % 2], 16)

            def load_quad(i, q):
                if q == 0:
                    sp.wait_ge(parts_out[0], parts_stored(i, 4))
                    wait_apart(sp, parts_out[1], parts_stored(i, 3))
                if not (isinstance(i, int) and i == 0):
                    wait_apart(sp, S["st_ps"], (i - 1) * 32 + 8 * q + 8)
                h = 4 * q
                for stack, base, groups in ((Ks, NH, ((0, 3, 0), (3, 2, 0), (5, 1, 0))), (Qs, 0, None)):
                    if groups:
                        for g, n, p in groups:
                            src = qk_d[base + h:base + h + 4, p:p + n].rearrange("h p d t -> (p d) h t")
                            sp.dma_start(stack[g * HD:(g + n) * HD, h:h + 4, :], src).then_inc(qin[q], 16)
                    else:
                        for g, p in enumerate((0, 0, 0, 1, 1, 2)):
                            src = qk_d[base + h:base + h + 4, p].rearrange("h d t -> d h t")
                            sp.dma_start(stack[g * HD:(g + 1) * HD, h:h + 4, :], src).then_inc(qin[q], 16)

            def load_max(i, q):
                wait_apart(sp, S["mT_sb"], i * 4 + q + 1)
                sp.dma_start(Qs[KROWS:KROWS + NPART, 4 * q:4 * q + 4, :], mTs[:, q % 2, :]).then_inc(m_in[q % 2], 16)

            def store_xn(i):
                sp.wait_ge(S["nHi"], i * 4 + 4)
                wait_apart(sp, S["nLo"], i * 2 + 2)
                sp.dma_start(xn_d[i, :, 0:2, :], Nh[:, 0:2, :].bitcast(F32)).then_inc(S["xn_out"], 16)
                sp.dma_start(xn_d[i, :, 2:4, :], Nl[:].bitcast(F32)).then_inc(S["xn_out"], 16)
                sp.dma_start(xn_d[i, 0:STACK, 4, :], Nh[0:STACK, 2, :].bitcast(F32)).then_inc(S["xn_out"], 16)

            load_front(0)
            load_front(1)
            store_parts(0)
            for q in range(4):
                load_quad(0, q)

            def sequence(i, first=False, second=False, last=False):
                if not (first or last):
                    load_front(i + 1)
                if not first:
                    load_max(i - 1, 3)
                    load_quad(i, 2)
                load_max(i, 0)
                if not (first or second):
                    store_xn(i - 2)
                if not first:
                    load_quad(i, 3)
                    load_tail(i - 1)
                load_max(i, 1)
                if not last:
                    store_parts(i + 1, (0, 1))
                load_max(i, 2)
                if not last:
                    store_parts(i + 1, (2, 3, 4))
                    load_quad(i + 1, 0)
                    load_quad(i + 1, 1)

            def load_expert(e):
                for t in range(HT):
                    if not (isinstance(e, int) and e == 0):
                        wait_apart(sp, S["w_hi"], e * HT * 2)
                        wait_apart(sp, S["w_lo"], e * HT * 3)
                    cols = slice(t * 128, (t + 1) * 128)
                    sp.dma_start(wr[:, t, 0:2, :], w1[e, 0:256, cols].rearrange("(c p) n -> p c n", p=128)).then_inc(wraw[t], 16)
                    for r in range(3):
                        sp.dma_start(wr[32 * r:32 * r + 32, t, 2, :], w1[e, 256:C, cols]).then_inc(wraw[t], 16)
                    sp.dma_start(vr[:, t, :], w2[e, cols, :]).then_inc(wraw[t], 16)

            sequence(0, first=True)
            sequence(1, second=True)
            with sp.Fori(2, NB - 1) as i:
                sequence(i)
            sequence(NB - 1, last=True)
            load_max(NB - 1, 3)
            store_xn(NB - 2)
            load_tail(NB - 1)
            sp.wait_ge(S["st_ps"], NB * 32)
            sp.wait_ge(S["av_ps"], NB * 32)
            sp.wait_ge(S["v_sb"], NB * NT)
            load_expert(0)
            store_xn(NB - 1)
            sp.wait_ge(S["xn_out"], NB * 48)
            sp.wait_ge(S["x2_2"], NB * NT)
            sp.dma_start(b1s[:], b1T).then_inc(S["ld_b1"], 16)

            def group_loads(e, pair, u, peeled=False):
                b = pair * 2 + u
                if not peeled:
                    g1 = e * NB + pair * 2 + (u - 1)
                    wait_apart(sp, S["m1_ps"], g1 * HT)
                    wait_apart(sp, S["eg"], g1 * NT)
                sp.dma_start(xn[:, u, 0:4, :].bitcast(F32), xn_d[b, :, 0:4, :]).then_inc(ld_xn[u], 16)
                sp.dma_start(xn[0:STACK, u, 4, :].bitcast(F32), xn_d[b, 0:STACK, 4, :]).then_inc(ld_xn[u], 16)
                sp.dma_start(gc[:, u, :], gate_d[b, 1, :].partition_broadcast(128)).then_inc(ld_gc[u], 16)

            group_loads(0, 0, 0, peeled=True)
            group_loads(0, 0, 1, peeled=True)
            load_expert(1)
            with sp.Fori(1, NB // 2) as p:
                for u in range(2):
                    group_loads(0, p, u)
            with sp.Fori(1, NE - 1) as e:
                with sp.Fori(0, NB // 2) as p:
                    for u in range(2):
                        group_loads(e, p, u)
                load_expert(e + 1)
            with sp.Fori(0, NB // 2) as p:
                for u in range(2):
                    group_loads(NE - 1, p, u)
            with sp.Fori(0, NB) as b:
                wait_apart(sp, S["acc"], ((NE - 1) * NB) * NT + (b + 1) * NT)
                sp.dma_start(out[b].rearrange("(t p) c -> p t c", p=128), X2[:, b]).then_inc(yout, 16)
            sp.wait_ge(yout, NB * 16)

        @block.gpsimd
        def _(pool):
            chain = [0]

            def link(ins):
                chain[0] += 1
                ins.then_inc(S["pch"], 1)
                pool.wait_ge(S["pch"], chain[0])

            link(pool.memset(ident[:], 0.0))
            link(pool.affine_select(out=ident[:], in_=ident[:], compare_op=ALU.not_equal, fill=1.0, base=0,
                                    pattern=[[-1, 128]], channel_multiplier=1))
            link(pool.tensor_copy(identb[:], ident[:]))
            link(pool.memset(ones[:], 1.0))
            link(pool.memset(nhalf[:], -0.5))
            link(pool.memset(modt[:], 0.0))
            link(pool.memset(maskge[:], 1.0))
            link(pool.affine_select(out=maskge[:], in_=maskge[:], compare_op=ALU.is_ge, fill=0.0, base=0,
                                    pattern=[[-1, D]], channel_multiplier=1))
            link(pool.memset(striu[:], 1.0))
            link(pool.affine_select(out=striu[:], in_=striu[:], compare_op=ALU.is_gt, fill=0.0, base=0,
                                    pattern=[[1, D]], channel_multiplier=-1))
            for t in range(NSQ):
                pool.memset(pw[:, 0, t:t + 1], 2.0 ** t).then_inc(S["pch"], 1)
                pool.memset(pw[:, 1, t:t + 1], 2.0 ** -(t + 1)).then_inc(S["pch"], 1)
            chain[0] += 2 * NSQ
            pool.wait_ge(S["pch"], chain[0])
            pool.memset(sc[:, 15:16], 0.0).then_inc(S["const"], 1)
            pool.wait_ge(S["s_silu"], 2)
            pool.tensor_tensor(sT[:], cT[:], eT[:], ALU.mult).then_inc(S["s_silu"], 1)
            pool.wait_ge(S["up_in"], 16)
            pool.wait_ge(S["ld_bU"], 16)
            pool.tensor_tensor(Ab[:], Ab[:], bc(bUs[:].unsqueeze(1), [D, NB, D]), ALU.add).then_inc(S["expm_pool"], 1)
            pool.wait_ge(S["expm_dve"], FLAGS_DONE)
            pool.tensor_tensor(dg[:], bc(ident[0:NB, 0:NB].unsqueeze(2), [NB, NB, NSQ + 1]),
                               bc(fs[:].unsqueeze(1), [NB, NB, NSQ + 1]), ALU.mult).then_inc(S["expm_pool"], 1)
            pool.wait_ge(S["ld_wq"], 128)
            pool.tensor_copy(wqh[:, 0:2, :], wqr[:, 0:2, :]).then_inc(S["wq_split"], 1)
            pool.tensor_copy(wqh[0:STACK, 2, :], wqr[0:STACK, 2, :]).then_inc(S["wq_split"], 1)
            pool.tensor_copy(wgh[:, 0:2, :], wgr[:, 0:2, :]).then_inc(S["wq_split"], 1)
            pool.tensor_copy(wgh[0:STACK, 2, :], wgr[0:STACK, 2, :]).then_inc(S["wq_split"], 1)
            pool.wait_ge(S["wq_split"], 4)
            link(pool.tensor_tensor(wql[:], wqr[:, 0:2, :], wqh[:, 0:2, :].bitcast(F32), ALU.subtract))
            link(pool.tensor_tensor(wgl[:], wgr[:, 0:2, :], wgh[:, 0:2, :].bitcast(F32), ALU.subtract))
            link(pool.tensor_tensor(wqh[64:96, 2, :], wqr[64:96, 2, :], wqh[64:96, 2, :].bitcast(F32), ALU.subtract))
            pool.tensor_tensor(wgh[64:96, 2, :], wgr[64:96, 2, :], wgh[64:96, 2, :].bitcast(F32), ALU.subtract)\
                .then_inc(S["wq_split"], 1)
            pool.wait_ge(S["sq_ready"], 2 * NSQ)
            pool.tensor_tensor(RT[:], RT[:], bc(ident[0:D, 0:D].unsqueeze(1), [D, NB, D]), ALU.subtract).then_inc(S["rotm"], 1)
            pool.wait_ge(S["rot_out"], 16)
            pool.wait_ge(S["mod_out"], 16)
            pool.wait_ge(S["gate_out"], 16)
            pool.wait_ge(S["p_rot"], NB)
            pool.memset(Ks[96:128], 1.0).then_inc(S["kones"], 1)
            pool.wait_ge(S["kones"], 1)
            pool.memset(Va[:, :, :, HD:HD + 1], 1.0).then_inc(S["vones"], 1)
            pool.wait_ge(S["vones"], 1)
            pool.memset(Va[:, :, :, HD + 1:VW], 0.0).then_inc(S["vones"], 1)

            def eps_pow(i, k, mean_sem, out_sem, chain_sem):
                wait_apart(pool, mean_sem, i * NT + NT)
                pool.tensor_scalar(ve[:, k], mv[:, k, :, 1], 1.0, 1e-6, ALU.mult, ALU.add).then_inc(chain_sem, 1)
                wait_apart(pool, chain_sem, i + 1)
                pool.tensor_tensor(rstd[:, k], ve[:, k], nhalf[:], ALU.pow).then_inc(out_sem, 1)

            def split_front(i):
                for c in range(3):
                    rows = 128 if c < 2 else STACK
                    wait_apart(pool, S["hF"], i * 3 + c + 1)
                    if c == 0 and not fixed(i, 0):
                        wait_apart(pool, S["v_ps"], i * NT)
                    pool.tensor_copy(Hh[0:rows, c, :], F[0:rows, c, :]).then_inc(S["hHi"], 1)
                pool.wait_ge(S["hHi"], i * 4 + 3)
                pool.tensor_tensor(Hh[32:64, 2, :], F[32:64, 2, :], Hh[32:64, 2, :].bitcast(F32), ALU.subtract)\
                    .then_inc(S["hHi"], 1)
                pool.wait_ge(S["hHi"], i * 4 + 4)

            def last_parts(i, tiles=range(MT)):
                for m in tiles:
                    pool.wait_ge(S["qkm"], i * MT + m + 1)
                    pool.tensor_tensor(prt[0:MROWS[m], m % 2, 2, :], QF[0:MROWS[m], m % 2, :],
                                       prt[0:MROWS[m], m % 2, 1, :], ALU.subtract).then_inc(S["qkl"], 1)

            def split_expert(e, tiles=range(HT)):
                for t in tiles:
                    wait_apart(pool, wraw[t], e * 80 + 80)
                    if not (isinstance(e, int) and e == 0):
                        wait_apart(pool, S["m2_ps"], (e * NB - 1) * HT + (t + 1))
                    pool.tensor_copy(w1h[:, t, 0:2, :], wr[:, t, 0:2, :]).then_inc(S["w_hi"], 1)
                    pool.tensor_copy(w1h[0:STACK, t, 2, :], wr[0:STACK, t, 2, :]).then_inc(S["w_free"], 1)
                    pool.tensor_copy(w2h[:, t, :], vr[:, t, :]).then_inc(S["w_hi"], 1)
                    pool.wait_ge(S["w_hi"], e * (2 * HT) + (2 * t + 2))
                    pool.wait_ge(S["w_free"], e * HT + (t + 1))
                    pool.tensor_tensor(w1l[:, t], wr[:, t, 0:2, :], w1h[:, t, 0:2, :].bitcast(F32), ALU.subtract)\
                        .then_inc(S["w_lo"], 1)
                    pool.wait_ge(S["w_lo"], e * (3 * HT) + (3 * t + 1))
                    pool.tensor_tensor(w1h[64:96, t, 2, :], wr[64:96, t, 2, :], w1h[64:96, t, 2, :].bitcast(F32),
                                       ALU.subtract).then_inc(S["w_lo"], 1)
                    pool.wait_ge(S["w_lo"], e * (3 * HT) + (3 * t + 2))
                    pool.tensor_tensor(w2l[:, t, :], vr[:, t, :], w2h[:, t, :].bitcast(F32), ALU.subtract)\
                        .then_inc(S["w_lo"], 1)

            def split_tail(i):
                for c in range(3):
                    rows = 128 if c < 2 else STACK
                    wait_apart(pool, S["nF"], i * 3 + c + 1)
                    if c == 0 and not fixed(i, 0):
                        pool.wait_ge(S["xn_out"], i * 48)
                        wait_apart(pool, S["gl_ps"], i)
                    pool.tensor_copy(Nh[0:rows, c, :], F[0:rows, c, :]).then_inc(S["nHi"], 1)
                pool.wait_ge(S["nHi"], i * 4 + 3)
                pool.tensor_tensor(Nh[32:64, 2, :], F[32:64, 2, :], Nh[32:64, 2, :].bitcast(F32), ALU.subtract)\
                    .then_inc(S["nHi"], 1)
                pool.wait_ge(S["nHi"], i * 4 + 4)

            def sequence(i, first=False, second=False, last=False):
                for h in range(NH):
                    if h == NT_AT and not (first or second):
                        split_tail(i - 2)
                    if h == NORM_AT and not last:
                        eps_pow(i + 1, 0, S["mvf"], S["rstd_f"], S["var_eps"])
                    if h == HT_AT and not last:
                        split_front(i + 1)
                    if h in QK_AT and not last:
                        last_parts(i + 1, QK_AT[h])
                    if h == NORM2_AT and not first:
                        eps_pow(i - 1, 1, S["mvn"], S["rstd_n"], S["var_eps2"])

            eps_pow(0, 0, S["mvf"], S["rstd_f"], S["var_eps"])
            split_front(0)
            last_parts(0)
            sequence(0, first=True)
            sequence(1, second=True)
            with pool.Fori(2, NB - 1) as i:
                sequence(i)
            sequence(NB - 1, last=True)
            split_tail(NB - 2)
            split_expert(0, range(0, 3))
            eps_pow(NB - 1, 1, S["mvn"], S["rstd_n"], S["var_eps2"])
            split_tail(NB - 1)
            split_expert(0, range(3, HT))
            with pool.Fori(1, NE) as e:
                split_expert(e)

        @block.scalar
        def _(act):
            act.wait_ge(S["ld_cond"], 16)
            act.activation(eT[:], cT[:], ACT.Exp, scale=-1.0).then_inc(S["e_silu"], 1)

            def side(k):
                for n in range(8):
                    if k == vf_step(3 * n + 2):
                        act.wait_ge(S["p_vf"], n + 1)
                        act.activation(vf[:, n * 512:(n + 1) * 512], bank[2 + n % 2][0:NB, :], ACT.Copy).then_inc(S["vf_ready"], 1)
                if k == MODS_AT[-1]:
                    act.wait_ge(S["p_mods"], 1)
                    for s in range(4):
                        for c, rows in ((slice(0, 2), 128), (slice(2, 3), STACK)):
                            n = c.stop - c.start
                            src = bank[5][0:rows, s * 24 + c.start * 8:s * 24 + c.stop * 8].rearrange("p (c b) -> p c b", b=NB)
                            dst = modt[0:rows, :, 3 * s + c.start:3 * s + c.stop].rearrange("p b c -> p c b")
                            act.activation(dst, src, ACT.Copy, bias=float(s % 2)).then_inc(S["mods"], 1)
                if k in GATES_AT:
                    g = GATES_AT.index(k)
                    act.wait_ge(S["p_gates"], g + 1)
                    act.activation(gts[:, g, :], bank[6 + g][0:NB, 0:C], ACT.Copy).then_inc(S["gates"], 1)
                if k == 24:
                    act.wait_ge(S["expm_ps"], PS_FS)
                    act.activation(fsb[:], bank[4][0:D, 0:NB * (NSQ + 1)].rearrange("p (b t) -> p b t", b=NB),
                                   ACT.Copy).then_inc(S["expm_act"], 1)
                if k == 26:
                    act.wait_ge(S["expm_ps"], PS_A2)
                    act.activation(A2[:], bank[2][0:D].rearrange("p (b j) -> p b j", b=NB), ACT.Copy, scale=-1.0)\
                        .then_inc(S["expm_act"], 1)
                if k == 27:
                    act.wait_ge(S["expm_ps"], PS_A3)
                    act.activation(A3[:], bank[3][0:D].rearrange("p (b j) -> p b j", b=NB), ACT.Copy)\
                        .then_inc(S["expm_act"], 1)
                    act.wait_ge(S["expm_ps"], PS_A4)
                    act.activation(A4[:], bank[4][0:D].rearrange("p (b j) -> p b j", b=NB), ACT.Copy)\
                        .then_inc(S["expm_act"], 1)
                if k == 30:
                    act.wait_ge(S["expm_ps"], PS_RT)
                    act.activation(RT[:], bank[4][0:D].rearrange("p (b j) -> p b j", b=NB), ACT.Copy)\
                        .then_inc(S["expm_act"], 1)
            for j in range(D):
                act.wait_ge(S["qrD"], j + 1)
                act.activation(sc[:, 0:1], R[0][0:CH, j:j + 1], ACT.Sqrt).then_inc(S["sigma"], 1)
                side(j)
                if j + 1 < D:
                    act.wait_ge(S["upd"], 3 * j + 1)
                    act.activation(a0m[:, (j + 1) % 2:(j + 1) % 2 + 1], A[:, 0, j + 1:j + 2], ACT.Identity,
                                   scale=maskge[:, j + 1:j + 2]).then_inc(S["a0"], 1)
            act.wait_ge(S["expm_ps"], PS_VT)
            act.activation(VT[:], bank[2][0:D, 0:C], ACT.Copy).then_inc(S["expm_act"], 1)
            act.wait_ge(S["expm_ps"], PS_XT)
            act.activation(XX[:, 1, :], bank[3][0:D, 0:D], ACT.Copy).then_inc(S["XT_ready"], 1)
            for k in range(5):
                act.wait_ge(S["p_X"], k + 1)
                act.activation(XX[:], bank[4][0:D, 0:2 * D].rearrange("p (k j) -> p k j", k=2), ACT.Copy)\
                    .then_inc(S["XT_ready"], 1)
            for b in range(NB):
                act.wait_ge(S["p_rot"], b + 1)
                act.activation(Gs[:, b, :], bank[b][0:D, 0:C], ACT.Copy).then_inc(S["rot_ready"], 1)


            def xT_out(i):
                for c in range(NCH):
                    act.wait_ge(S["xT_ps"], i * 3 + c + 1)
                    act.activation(xT[:, c, :], R[c % 2][0:CH, :], ACT.Copy).then_inc(S["xT_sb"], 1)

            def z_out(i):
                act.wait_ge(S["z_ps"], i + 1)
                act.activation(zT[:], R[1][0:D, :], ACT.Copy).then_inc(S["z_sb"], 1)

            def hT_out(i, nosplit=False):
                act.wait_ge(S["ld_modf"], i * 16 + 16)
                for c in range(3):
                    rows = 128 if c < 2 else STACK
                    act.wait_ge(S["hT_ps"], i * 3 + c + 1)
                    if c == 0 and not fixed(i, 0):
                        act.wait_ge(S["hHi"], i * 4)
                        act.wait_ge(S["hLo"], i * 2)
                        if not fixed(i, 1):
                            act.wait_ge(S["nHi"], (i - 2) * 4)
                            act.wait_ge(S["nLo"], (i - 2) * 2)
                    act.activation(F[0:rows, c, :], R[c % 2][0:rows, :], ACT.Identity, scale=modf[0:rows, 3 + c:4 + c],
                                   bias=modf[0:rows, c:c + 1]).then_inc(S["hF"], 1)

            def qk_out(i, tiles=range(MT)):
                for m in tiles:
                    rows = MROWS[m]
                    act.wait_ge(S["qk_ps"], i * MT + m + 1)
                    if m >= 2:
                        act.wait_ge(S["qkl"], i * MT + (m - 1))
                        act.wait_ge(parts_out[m % 2], parts_stored(i, m - 2))
                    elif not fixed(i, 0):
                        act.wait_ge(S["qkl"], i * MT)
                        act.wait_ge(parts_out[m % 2], parts_stored(i - 1, 4 - m % 2))
                    src = R[(m + 1) % 2][0:rows, :]
                    act.activation(QF[0:rows, m % 2, :], src, ACT.Identity, bias=bqk[0:rows, m:m + 1]).then_inc(S["qkF"], 1)
                    act.activation(prt[0:rows, m % 2, 0, :], src, ACT.Identity, bias=bqk[0:rows, m:m + 1])\
                        .then_inc(S["qkh"], 1)

            def mT_out(i, q):
                act.wait_ge(S["mT_ps"], i * 4 + q + 1)
                if q >= 2 or not fixed(i, 0):
                    act.wait_ge(m_in[q % 2], (i * 2 + q // 2) * 16)
                act.activation(mTs[:, q % 2, :], R[0][0:48, 0:64].bitcast(BF16), ACT.Copy).then_inc(S["mT_sb"], 1)

            def exps(i, h, k):
                act.wait_ge(S["st_ps"], i * 32 + (2 * h + k + 1))
                if h >= 2 or not fixed(i, 0):
                    act.wait_ge(S["av_ps"], i * 32 + (2 * (h - 2) + k + 1))
                act.activation(PT[:, h % 2, 2 * k:2 * k + 2, :], ST[k][:], ACT.Exp, scale=SCALE)\
                    .then_inc(S["expd"], 1)

            def av_out(i, h):
                act.wait_ge(S["av_ps"], i * 32 + (2 * h + 2))
                if h or not fixed(i, 0):
                    act.wait_ge(S["tok_ps"], i * NH + h)
                act.activation(oTh[:], OB[0][0:VW, :], ACT.Copy).then_inc(S["avT"], 1)

            def oT_out(i):
                for c in range(NCH):
                    act.wait_ge(S["oT_ps"], i * 3 + c + 1)
                    act.activation(xT[:, c, :], R[c % 2][0:CH, :], ACT.Copy).then_inc(S["oT_sb"], 1)

            def nT_out(i):
                act.wait_ge(S["ld_modn"], i * 16 + 16)
                for c in range(3):
                    rows = 128 if c < 2 else STACK
                    act.wait_ge(S["nT_ps"], i * 3 + c + 1)
                    if c == 0:
                        act.wait_ge(S["nHi"], i * 4)
                        act.wait_ge(S["nLo"], i * 2)
                        fronts = i + 3 if not isinstance(i, int) else min(i + 3, NB)
                        act.wait_ge(S["hHi"], fronts * 4)
                        act.wait_ge(S["hLo"], fronts * 2)
                    act.activation(F[0:rows, c, :], R[c % 2][0:rows, :], ACT.Identity,
                                   scale=modn[0:rows, 9 + c:10 + c], bias=modn[0:rows, 6 + c:7 + c]).then_inc(S["nF"], 1)

            def gate_exp(i):
                act.wait_ge(S["top"], i + 1)
                act.activation(m12[:, 3, :], m12[:, 2, :], ACT.Exp).then_inc(S["g_exp"], 1)

            def cwT_out(i):
                act.wait_ge(S["cwT_ps"], i + 1)
                act.activation(zT[0:NE, :], R[0][0:NE, :], ACT.Copy).then_inc(S["cwT_sb"], 1)

            def sequence(i, first=False, second=False, last=False):
                for h in range(NH):
                    if h == GATE_AT + 2 and not (first or second):
                        gate_exp(i - 2)
                    st, av = behind(i, h, 8, first), behind(i, h, 10, first)
                    if st:
                        exps(*st, 0)
                    if av:
                        av_out(*av)
                    if st:
                        exps(*st, 1)
                    if h % 4 == 0 and (h or not first):
                        mT_out(*quad_before(i, h))
                    if h == XT_AT and not last:
                        xT_out(i + 1)
                    if h == NT_AT and not (first or second):
                        nT_out(i - 2)
                    if h == Z_AT and not last:
                        z_out(i + 1)
                    if h == CW_AT and not (first or second):
                        cwT_out(i - 2)
                    if h == HT_AT and not last:
                        hT_out(i + 1)
                    if h == OT_AT and not first:
                        oT_out(i - 1)
                    if h in QK_AT and not last:
                        qk_out(i + 1, QK_AT[h])

            xT_out(0)
            z_out(0)
            act.wait_ge(S["rot_out"], 16)
            act.wait_ge(S["ld_misc"], 16 * (4 + MT))
            act.wait_ge(S["wq_split"], 5)
            hT_out(0)
            qk_out(0)
            sequence(0, first=True)
            sequence(1, second=True)
            with act.Fori(2, NB - 1) as i:
                sequence(i)
            sequence(NB - 1, last=True)
            for h in range(8, NH + 2):
                if h == 8 + GATE_AT + 2:
                    gate_exp(NB - 2)
                if h < NH:
                    exps(NB - 1, h, 0)
                av_out(NB - 1, h - 2)
                if h < NH:
                    exps(NB - 1, h, 1)
                if h == 8:
                    mT_out(NB - 1, 3)
                if h == 8 + NT_AT:
                    nT_out(NB - 2)
                if h == 8 + CW_AT:
                    cwT_out(NB - 2)
            oT_out(NB - 1)
            nT_out(NB - 1)
            gate_exp(NB - 1)
            cwT_out(NB - 1)
            act.wait_ge(S["x2_2"], NB * NT)
            act.wait_ge(S["xn_out"], NB * 48)
            act.wait_ge(S["ld_b1"], 16)

            def gelus(e, g, later):
                for t in range(HT):
                    act.wait_ge(S["m1_ps"], g * HT + (t + 1))
                    if later or t >= 3:
                        act.wait_ge(S["ghi"], g * HT + (t - 2))
                        act.wait_ge(S["glo"], g * HT + (t - 2))
                    act.activation(GF[:, t % 3, :], m1_bank(t),
                                   ACT.Gelu_apprx_tanh, bias=b1s[:, e * HT + t:e * HT + t + 1] if isinstance(e, int)
                                   else b1s[:, bass.ds(e * HT + t, 1)]).then_inc(S["gelu"], 1)
                    act.wait_ge(S["gelu"], g * HT + (t + 1))
                    if later or t >= 3:
                        act.wait_ge(S["m2_ps"], g * HT + (t - 2))
                    act.activation(Gh[:, t % 3, :], GF[:, t % 3, :], ACT.Copy).then_inc(S["ghi"], 1)

            gelus(0, 0, False)
            with act.Fori(1, NB) as g:
                gelus(0, g, True)
            with act.Fori(1, NE) as e:
                with act.Fori(0, NB) as b:
                    gelus(e, e * NB + b, True)

        @block.vector
        def _(v):
            chain = [0]

            def link(ins):
                chain[0] += 1
                ins.then_inc(S["dch"], 1)
                v.wait_ge(S["dch"], chain[0])

            v.wait_ge(S["const"], 1)
            v.wait_ge(S["e_silu"], 1)
            v.tensor_scalar(eT[:], eT[:], 1.0, None, ALU.add).then_inc(S["s_silu"], 1)
            v.wait_ge(S["s_silu"], 1)
            v.reciprocal(eT[:], eT[:]).then_inc(S["s_silu"], 1)

            I8 = bc(ident[0:D, 0:D].unsqueeze(1), [D, NB, D])

            def poly(k, dst):
                c = TAYLOR[4 * k:4 * k + 4]
                link(v.tensor_scalar(dst[:], A3[:], c[3], None, ALU.mult))
                link(v.scalar_tensor_tensor(dst[:], A2[:], c[2], dst[:], ALU.mult, ALU.add))
                link(v.scalar_tensor_tensor(dst[:], Ab[:], c[1], dst[:], ALU.mult, ALU.add))
                return v.scalar_tensor_tensor(dst[:], I8, c[0], dst[:], ALU.mult, ALU.add)

            def view8(b):
                return b[0:D].rearrange("p (b j) -> p b j", b=NB)

            def side(k):
                if k == 22:
                    v.wait_ge(S["expm_ps"], PS_UPT)
                    v.tensor_tensor(Ab[:], Ab[:], view8(bank[2]), ALU.subtract).then_inc(S["expm_dve"], 1)
                    v.wait_ge(S["expm_dve"], SKEW_DONE)
                    v.tensor_reduce(rs[:], Ab[:], AX.X, ALU.add, apply_absolute_value=True).then_inc(S["expm_dve"], 1)
                if k == 23:
                    v.wait_ge(S["expm_ps"], PS_RST)
                    link(v.tensor_reduce(nrm[:, 0:1], bank[3][0:NB, 0:D], AX.X, ALU.max))
                    link(v.tensor_scalar(fs[:, 0:NSQ], pw[:, 0, :], nrm[:, 0:1], None, ALU.is_lt))
                    link(v.tensor_tensor(fq[:], fs[:, 0:NSQ], pw[:, 1, :], ALU.mult))
                    link(v.tensor_reduce(nrm[:, 1:2], fq[:], AX.X, ALU.add))
                    v.tensor_scalar(fs[:, NSQ:NSQ + 1], nrm[:, 1:2], -1.0, 1.0, ALU.mult, ALU.add).then_inc(S["expm_dve"], 1)
                if k == 25:
                    v.wait_ge(S["expm_act"], FLAGS_SPREAD)
                    v.tensor_tensor(Ab[:], Ab[:], bc(fsb[:, :, NSQ:NSQ + 1], [D, NB, D]), ALU.mult).then_inc(S["expm_dve"], 1)
                if k == 28:
                    v.wait_ge(S["expm_act"], A3_DONE)
                    v.wait_ge(S["expm_act"], A2_DONE)
                    v.wait_ge(S["expm_dve"], SCALED_DONE)
                    poly(2, Bk).then_inc(S["expm_dve"], 1)
                    link(poly(1, L))
                    v.wait_ge(S["expm_ps"], PS_H1)
                    v.tensor_tensor(L[:], L[:], view8(bank[2]), ALU.add).then_inc(S["expm_dve"], 1)
                    link(poly(0, RR))
                if k == 29:
                    v.wait_ge(S["expm_ps"], PS_H2)
                    v.tensor_tensor(RR[:], RR[:], view8(bank[3]), ALU.add).then_inc(S["expm_dve"], 1)

            def square(t):
                v.wait_ge(S["p_sq"], 2 * t + 2)
                flag = bc(fsb[:, :, t:t + 1].bitcast(mybir.dt.int32), [D, NB, D])
                for dst, src in ((RR, bank[2]), (RT, bank[3])):
                    v.copy_predicated(dst[:], flag, view8(src)).then_inc(S["sq_ready"], 1)

            v.wait_ge(S["ld_P"], 16)
            v.tensor_tensor(a0m[:, 0:1], A[:, 0, 0:1], maskge[:, 0:1], ALU.mult).then_inc(S["a0"], 1)
            sig, g2, nb, w, al, rc = (sc[:, k:k + 1] for k in range(6))
            for j in range(D):
                am = a0m[:, j % 2:j % 2 + 1]

                def signal(ins):
                    chain[0] += 1
                    ins.then_inc(S["dch"], 1)

                v.wait_ge(S["qrE"], j + 1)
                link(v.tensor_copy(Es[:, j:D], R[1][0:CH, j:D]))
                link(v.tensor_scalar(g2, Es[:, j:j + 1], 0.0, 2.0, ALU.is_ge, ALU.mult))
                signal(v.scalar_tensor_tensor(al, g2, -1.0, Es[:, j:j + 1], ALU.add, ALU.mult))
                v.wait_ge(S["sigma"], j + 1)
                v.wait_ge(S["dch"], chain[0])
                signal(v.scalar_tensor_tensor(nb, g2, -1.0, sig, ALU.add, ALU.mult))
                link(v.scalar_tensor_tensor(w, al, sig, R[0][0:CH, j:j + 1], ALU.mult, ALU.add))
                signal(v.reciprocal(rc, w))
                if j + 1 < D:
                    signal(v.scalar_tensor_tensor(t1[:, j + 1:D], Es[:, j + 1:D], nb, R[0][0:CH, j + 1:D],
                                                  ALU.mult, ALU.add))
                if j + 1 < D:
                    v.wait_ge(S["dch"], chain[0])
                    signal(v.tensor_scalar(cc[:, j + 1:D], t1[:, j + 1:D], rc, -1.0, ALU.mult, ALU.mult))
                v.wait_ge(S["a0"], j + 1)
                link(v.scalar_tensor_tensor(V0[:, j:j + 1], ident[0:CH, j:j + 1], nb, am, ALU.mult, ALU.add))
                if j + 1 < D:
                    for t in range(NCH):
                        vj = V0[:, j:j + 1] if t == 0 else A[:, t, j:j + 1]
                        v.scalar_tensor_tensor(A[:, t, j + 1:D], cc[:, j + 1:D], vj, A[:, t, j + 1:D],
                                               ALU.mult, ALU.add).then_inc(S["upd"], 1)
                side(j)
                if SQ0 < j < SQ0 + 2 * NSQ and (j - SQ0) % 2:
                    square((j - SQ0) // 2)
            v.wait_ge(S["dch"], chain[0])
            v.tensor_copy(A[:, 0, :], V0[:]).then_inc(S["V_ready"], 1)
            v.wait_ge(S["expm_ps"], PS_S)
            link(v.tensor_tensor_reduce(out=Y[:], in0=R[0][0:D, 0:D], in1=ident[0:D, 0:D], scale=1.0, scalar=0.0,
                                        op0=ALU.mult, op1=ALU.add, accum_out=dd[:, 0:1]))
            link(v.reciprocal(dd[:, 1:2], dd[:, 0:1]))
            link(v.tensor_scalar(dd[:, 2:3], dd[:, 1:2], -2.0, None, ALU.mult))
            link(v.tensor_scalar(dd[:, 3:4], dd[:, 1:2], 2.0, None, ALU.mult))
            v.scalar_tensor_tensor(XX[:, 0, :], R[0][0:D, 0:D], dd[:, 2:3], striu[:], ALU.mult, ALU.mult)\
                .then_inc(S["expm_dve"], 1)
            v.wait_ge(S["expm_act"], VT_DONE)
            v.tensor_scalar(Y[:], VT[:, 0:D], dd[:, 3:4], None, ALU.mult).then_inc(S["Y_ready"], 1)
            for k in range(6):
                v.wait_ge(S["p_Y"], k + 1)
                v.tensor_tensor(Y[:], Y[:], bank[5][0:D, 0:D], ALU.add).then_inc(S["Y_ready"], 1)
            v.wait_ge(S["p_U"], 2)
            pu = bank[6][0:CH, 0:NCH * D].rearrange("p (t d) -> p t d", t=NCH)
            v.tensor_scalar(U[:, 1:NCH, :], pu[:, 1:NCH, :], -1.0, None, ALU.mult).then_inc(S["U_ready"], 1)
            v.scalar_tensor_tensor(U[:, 0, :], pu[:, 0, :], -1.0, ident[0:CH, 0:D], ALU.mult, ALU.add).then_inc(S["U_ready"], 1)
            v.tensor_scalar(UT[:, D:C], bank[7][0:D, D:C], -1.0, None, ALU.mult).then_inc(S["U_ready"], 1)
            v.scalar_tensor_tensor(UT[:, 0:D], bank[7][0:D, 0:D], -1.0, ident[0:D, 0:D], ALU.mult, ALU.add)\
                .then_inc(S["U_ready"], 1)

            v.wait_ge(S["rot_out"], 16)
            v.wait_ge(S["vones"], 2)

            def xrot(i):
                v.wait_ge(S["ld_x"], i * 16 + 16)
                for t in range(NT):
                    v.wait_ge(S["delta_ps"], i * NT + t + 1)
                    v.tensor_tensor(X2[:, i, t, :], R[t % 2][:, 0:C], xin[:, t, :], ALU.add).then_inc(S["xrot"], 1)
                for t in range(NT):
                    wait_apart(v, S["xrot"], i * NT + t + 1)
                    v.bn_stats(st6[:, 0, t, :], X2[:, i, t, :]).then_inc(S["bst"], 1)
                for t in range(NT):
                    wait_apart(v, S["bst"], i * NT + t + 1)
                    v.bn_aggr(mv[:, 0, t, :], st6[:, 0, t, :]).then_inc(S["mvf"], 1)

            def normalise(i, k, ready, done):
                v.wait_ge(ready, i + 1)
                for t in range(NT):
                    v.tensor_scalar(xh[:, t, 0:256], X2[:, i, t, 0:256], mv[:, k, t, 0:1], rstd[:, k, t:t + 1],
                                    ALU.subtract, ALU.mult).then_inc(done, 1)
                    last = X2[:, i, t, 256:C]
                    v.tensor_scalar(xh[:, t, 256:XW].rearrange("p (r n) -> p r n", r=3),
                                    bc(last.unsqueeze(1), [128, 3, 32]), mv[:, k, t, 0:1], rstd[:, k, t:t + 1],
                                    ALU.subtract, ALU.mult).then_inc(done, 1)

            def norm_front(i):
                if not fixed(i, 0):
                    v.wait_ge(S["hT_ps"], i * 3)
                    if not fixed(i, 1):
                        v.wait_ge(S["nT_ps"], (i - 2) * 3)
                normalise(i, 0, S["rstd_f"], S["xh_f1"])

            def h_lo(i):
                if not (isinstance(i, int) and i == 0):
                    v.wait_ge(S["v_ps"], i * NT)
                for c in range(2):
                    v.wait_ge(S["hHi"], i * 4 + c + 1)
                    v.tensor_tensor(Hl[:, c, :], F[:, c, :], Hh[:, c, :].bitcast(F32), ALU.subtract).then_inc(S["hLo"], 1)

            def qk_parts(i, tiles=range(MT)):
                for m in tiles:
                    rows, s = MROWS[m], m % 2
                    v.wait_ge(S["qkF"], i * MT + m + 1)
                    v.wait_ge(S["qkh"], i * MT + m + 1)
                    v.tensor_tensor(QF[0:rows, s, :], QF[0:rows, s, :], prt[0:rows, s, 0, :], ALU.subtract)\
                        .then_inc(S["qkr"], 1)
                    v.wait_ge(S["qkr"], i * MT + m + 1)
                    v.tensor_copy(prt[0:rows, s, 1, :], QF[0:rows, s, :]).then_inc(S["qkm"], 1)

            def v_out(i):
                v.wait_ge(S["av_ps"], i * 32)
                for t in range(NT):
                    v.wait_ge(S["v_ps"], i * NT + t + 1)
                    v.tensor_tensor(Va[:, t, :, 0:HD], R[t % 2][:, 0:C].rearrange("p (h d) -> p h d", h=NH),
                                    bv[:].rearrange("p (h d) -> p h d", h=NH), ALU.add).then_inc(S["v_sb"], 1)

            def maxima(i, h):
                q, s = h // 4, h % 4
                for t in range(NT):
                    v.wait_ge(S["s_ps"], i * 64 + (4 * h + t + 1))
                    v.tensor_reduce(mx[:, q, s, t:t + 1], R[t % 2][:], AX.X, ALU.max, negate=True).then_inc(S["smax"], 1)

            def max_parts(i, q):
                v.wait_ge(S["smax"], i * 64 + 16 * (q + 1))
                if q:
                    v.wait_ge(S["mT_ps"], i * 4 + q)
                else:
                    v.wait_ge(S["mT_ps"], i * 4)
                m = mx[:, q].rearrange("p h t -> p (h t)")
                first = i * 16 + 4 * q
                v.tensor_copy(mp[:, 0, :], m).then_inc(S["mparts"], 1)
                v.wait_ge(S["mparts"], first + 1)
                v.tensor_tensor(mr[:], m, mp[:, 0, :], ALU.subtract).then_inc(S["mparts"], 1)
                v.wait_ge(S["mparts"], first + 2)
                v.tensor_copy(mp[:, 1, :], mr[:]).then_inc(S["mparts"], 1)
                v.wait_ge(S["mparts"], first + 3)
                v.tensor_tensor(mp[:, 2, :], mr[:], mp[:, 1, :], ALU.subtract).then_inc(S["mparts"], 1)

            def o_out(i, p):
                v.wait_ge(S["tok_ps"], i * NH + 2 * p + 2)
                src = tok
                v.reciprocal(rec[:, p % 2], src[:, :, :, HD]).then_inc(S["orec"], 1)
                v.wait_ge(S["orec"], i * 8 + p + 1)
                if p == 0:
                    v.wait_ge(S["oT_ps"], i * 3)
                v.tensor_tensor(o[:, :, 2 * p * HD:2 * (p + 1) * HD].rearrange("p t (s d) -> p t s d", s=2),
                                src[:, :, :, 0:HD], bc(rec[:, p % 2].unsqueeze(3), [128, NT, 2, HD]), ALU.mult)\
                    .then_inc(S["o_sb"], 1)

            def x2_attn(i, tiles=range(NT)):
                v.wait_ge(S["ld_gat"], i * 16 + 16)
                for pair in range(min(tiles) // 2, max(tiles) // 2 + 1):
                    two, base = (2 * pair, 2 * pair + 1), i * 8 + 4 * pair
                    for t in two:
                        v.wait_ge(S["proj_ps"], i * NT + t + 1)
                        v.tensor_tensor(yt[:, t % 2, :], R[t % 2][:, 0:C], bp[:], ALU.add).then_inc(S["yg"], 1)
                    for t in two:
                        v.wait_ge(S["yg"], base + (t % 2 + 1))
                        v.tensor_tensor(yt[:, t % 2, :], yt[:, t % 2, :], gat[:, 0, :], ALU.mult).then_inc(S["yg"], 1)
                    for t in two:
                        v.wait_ge(S["yg"], base + (t % 2 + 3))
                        v.tensor_tensor(X2[:, i, t, :], X2[:, i, t, :], yt[:, t % 2, :], ALU.add).then_inc(S["x2_1"], 1)
                    for t in two:
                        wait_apart(v, S["x2_1"], i * NT + t + 1)
                        v.bn_stats(st6[:, 1, t, :], X2[:, i, t, :]).then_inc(S["bst2"], 1)
                for t in range(NT) if max(tiles) == NT - 1 else ():
                    wait_apart(v, S["bst2"], i * NT + t + 1)
                    v.bn_aggr(mv[:, 1, t, :], st6[:, 1, t, :]).then_inc(S["mvn"], 1)

            def norm_tail(i):
                v.wait_ge(S["nT_ps"], i * 3)
                fronts = i + 3 if not isinstance(i, int) else min(i + 3, NB)
                v.wait_ge(S["hT_ps"], fronts * 3)
                normalise(i, 1, S["rstd_n"], S["xh_n"])

            def n_lo(i):
                for c in range(2):
                    v.wait_ge(S["nHi"], i * 4 + c + 1)
                    v.tensor_tensor(Nl[:, c, :], F[:, c, :], Nh[:, c, :].bitcast(F32), ALU.subtract).then_inc(S["nLo"], 1)

            def seq(base, per, done=0):
                n = [done]

                def step(ins):
                    n[0] += 1
                    ins.then_inc(S["lgc"], 1)
                    v.wait_ge(S["lgc"], base * per + n[0])
                return step, n

            NLG = 20

            def first_of(step, mask, eq):
                step(v.tensor_copy(mask[:, :, 0:1], eq[:, :, 0:1]))
                step(v.tensor_scalar(us[:, :, 0:1], eq[:, :, 0:1], -1.0, 1.0, ALU.mult, ALU.add))
                for e in range(1, NE):
                    step(v.tensor_tensor(mask[:, :, e:e + 1], eq[:, :, e:e + 1], us[:, :, 0:1], ALU.mult))
                    if e + 1 < NE:
                        step(v.tensor_tensor(us[:, :, 0:1], us[:, :, 0:1], mask[:, :, e:e + 1], ALU.subtract))

            def first_expert(i):
                step, n = seq(i, NLG)
                v.wait_ge(S["gl_ps"], i + 1)
                step(v.tensor_copy(lg[:], R[0][:, 0:NT * NE].rearrange("p (t e) -> p t e", t=NT)))
                step(v.tensor_reduce(m12[:, 0, :], lg[:], AX.X, ALU.max))
                step(v.tensor_tensor(l2[:], lg[:], bc(m12[:, 0, :].unsqueeze(2), [128, NT, NE]), ALU.is_equal))
                first_of(step, k1, l2)
                assert n[0] == NLG // 2

            def second_expert(i):
                step, n = seq(i, NLG, NLG // 2)
                step(v.scalar_tensor_tensor(l2[:], k1[:], -3.0e38, lg[:], ALU.mult, ALU.add))
                step(v.tensor_reduce(m12[:, 1, :], l2[:], AX.X, ALU.max))
                step(v.tensor_tensor(l2[:], l2[:], bc(m12[:, 1, :].unsqueeze(2), [128, NT, NE]), ALU.is_equal))
                first_of(step, k2, l2)
                v.tensor_tensor(m12[:, 2, :], m12[:, 1, :], m12[:, 0, :], ALU.subtract).then_inc(S["top"], 1)
                assert n[0] == NLG

            def weights(i):
                v.wait_ge(S["g_exp"], i + 1)
                w = S["cw_ready"]
                v.tensor_scalar(m12[:, 0, :], m12[:, 3, :], 1.0, None, ALU.add).then_inc(w, 1)
                v.wait_ge(w, i * 6 + 1)
                v.reciprocal(m12[:, 1, :], m12[:, 0, :]).then_inc(w, 1)
                v.wait_ge(w, i * 6 + 2)
                v.tensor_tensor(k2[:], k2[:], bc(m12[:, 3, :].unsqueeze(2), [128, NT, NE]), ALU.mult).then_inc(w, 1)
                v.wait_ge(w, i * 6 + 3)
                v.tensor_tensor(k1[:], k1[:], k2[:], ALU.add).then_inc(w, 1)
                v.wait_ge(w, i * 6 + 4)
                v.tensor_tensor(cw[:, i], k1[:], bc(m12[:, 1, :].unsqueeze(2), [128, NT, NE]), ALU.mult).then_inc(w, 1)
                v.tensor_tensor(lg[:], k1[:], bc(m12[:, 1, :].unsqueeze(2), [128, NT, NE]), ALU.mult).then_inc(w, 1)

            def b2_add(i):
                for t in range(NT):
                    v.wait_ge(S["b2_ps"], i * NT + t + 1)
                    v.tensor_tensor(yt[:, t % 2, :], R[(t + 1) % 2][:, 0:C], gat[:, 1, :], ALU.mult).then_inc(S["b2g"], 1)
                    v.wait_ge(S["b2g"], i * NT + t + 1)
                    v.tensor_tensor(X2[:, i, t, :], X2[:, i, t, :], yt[:, t % 2, :], ALU.add).then_inc(S["x2_2"], 1)

            def sequence(i, first=False, second=False, last=False):
                for h in range(NH):
                    maxima(i, h)
                    if h % 4 == 3:
                        max_parts(i, h // 4)
                    if h in (12, 14):
                        o_out(i, (h - 12) // 2)
                    if h % 2 == 0 and h <= 10 and not first:
                        o_out(i - 1, h // 2 + 2)
                    if h == NT_AT + 1 and not (first or second):
                        n_lo(i - 2)
                    if h == DELTA_AT and not last:
                        xrot(i + 1)
                    if h == NORM_AT and not last:
                        norm_front(i + 1)
                    if GATE_AT <= h < GATE_AT + 3 and not (first or second):
                        (first_expert, second_expert, weights)[h - GATE_AT](i - 2)
                    if h == B2_AT and not (first or second):
                        b2_add(i - 2)
                    if h == V_AT:
                        v_out(i)
                    if h == HLO_AT and not last:
                        h_lo(i + 1)
                    if h in QK_AT and not last:
                        qk_parts(i + 1, QK_AT[h])
                    if h in PROJ_AT and not first:
                        x2_attn(i - 1, PROJ_AT[h])
                    if h == NORM2_AT and not first:
                        norm_tail(i - 1)

            xrot(0)
            norm_front(0)
            h_lo(0)
            qk_parts(0)
            sequence(0, first=True)
            sequence(1, second=True)
            with v.Fori(2, NB - 1) as i:
                sequence(i)
            sequence(NB - 1, last=True)
            for h in range(8, NH + 3):
                if h % 2 == 0:
                    o_out(NB - 1, h // 2 - 2)
                if h == 8 + NT_AT + 1:
                    n_lo(NB - 2)
                if 8 + GATE_AT <= h < 8 + GATE_AT + 3:
                    (first_expert, second_expert, weights)[h - 8 - GATE_AT](NB - 2)
                if h == 8 + B2_AT:
                    b2_add(NB - 2)
            x2_attn(NB - 1)
            norm_tail(NB - 1)
            n_lo(NB - 1)
            first_expert(NB - 1)
            second_expert(NB - 1)
            weights(NB - 1)
            b2_add(NB - 1)
            v.wait_ge(S["x2_2"], NB * NT)
            v.wait_ge(S["xn_out"], NB * 48)

            def group(e, pair, u, later):
                b, g = pair * 2 + u, pair * 2 + (e * NB + u)
                for t in range(HT):
                    v.wait_ge(S["ghi"], g * HT + (t + 1))
                    if later or t >= 3:
                        v.wait_ge(S["m2_ps"], g * HT + (t - 2))
                    v.tensor_tensor(Gl[:, t % 3, :], GF[:, t % 3, :], Gh[:, t % 3, :].bitcast(F32), ALU.subtract)\
                        .then_inc(S["glo"], 1)
                v.wait_ge(S["m2_ps"], (g + 1) * HT)
                v.wait_ge(ld_gc[u], (e * (NB // 2) + pair + 1) * 16)
                for t in range(NT):
                    if later:
                        v.wait_ge(S["acc"], (g - 1) * NT + (t + 1))
                    v.scalar_tensor_tensor(et[:, t, :], m2_bank(t)[:, 0:C], cw[:, b, t, e:e + 1], gc[:, u, :],
                                           ALU.mult, ALU.mult).then_inc(S["eg"], 1)
                for t in range(NT):
                    v.wait_ge(S["eg"], g * NT + (t + 1))
                    v.tensor_tensor(X2[:, b, t, :], X2[:, b, t, :], et[:, t, :], ALU.add).then_inc(S["acc"], 1)

            for u in range(2):
                group(0, 0, u, u > 0)
            with v.Fori(1, NB // 2) as p:
                for u in range(2):
                    group(0, p, u, True)
            for e in range(1, NE):
                with v.Fori(0, NB // 2) as p:
                    for u in range(2):
                        group(e, p, u, True)

        @block.tensor
        def _(pe):
            mm = pe.matmul

            def side(k):
                for piece in range(3 * 8):
                    if k != vf_step(piece):
                        continue
                    n, t = piece // 3, piece % 3
                    if t == 0:
                        pe.wait_ge(ld_wt[n % 4], 16 * (n // 4 + 1))
                        if n == 0:
                            pe.wait_ge(S["s_silu"], 3)
                        if n >= 2:
                            pe.wait_ge(S["vf_ready"], n - 1)
                    last = mm(bank[2 + n % 2][0:NB, :], sT[:, t, :], wts[:, n % 4, t, :], start=(t == 0), stop=(t == NCH - 1))
                    if t == NCH - 1:
                        last.then_inc(S["p_vf"], 1)
                if k in MODS_AT:
                    if k == MODS_AT[0]:
                        pe.wait_ge(S["ld_wad"], 16 * 26)
                    per = 12 // len(MODS_AT)
                    for n in range(per * MODS_AT.index(k), per * (MODS_AT.index(k) + 1)):
                        s, c = n // 3, n % 3
                        sec = (0, 1, 3, 4)[s]
                        rows = 128 if c < 2 else STACK
                        dst = bank[5][0:rows, s * 24 + c * 8:s * 24 + c * 8 + 8]
                        for t in range(NCH):
                            w = wad[:, t, sec * C + c * 128:sec * C + c * 128 + 128] if c < 2 else wad2[:, t, s, :]
                            mm(dst, w, sT[:, t, :], start=(t == 0), stop=False)
                        w = bad[:, sec * C + c * 128:sec * C + c * 128 + 128] if c < 2 else bad2[:, s, :]
                        last = mm(dst, w, ones[0:1, 0:NB], start=False, stop=True)
                    if k == MODS_AT[-1]:
                        last.then_inc(S["p_mods"], 1)
                if k in GATES_AT:
                    g = GATES_AT.index(k)
                    cols = slice((2 + 3 * g) * C, (3 + 3 * g) * C)
                    for t in range(NCH):
                        mm(bank[6 + g][0:NB, 0:C], sT[:, t, :], wad[:, t, cols], start=(t == 0), stop=False)
                    mm(bank[6 + g][0:NB, 0:C], ones[0:1, 0:NB], bad[:, cols], start=False, stop=True)\
                        .then_inc(S["p_gates"], 1)
                if k == 22:
                    pe.wait_ge(S["expm_pool"], UP_DONE)
                    pe.wait_ge(S["vf_ready"], 8)
                    for b in range(NB):
                        last = pe.transpose(bank[2][0:D, b * D:(b + 1) * D], Ab[:, b, :], ident[0:D, 0:D])
                    last.then_inc(S["expm_ps"], 1)
                    pe.wait_ge(S["expm_dve"], ROWSUM_DONE)
                    pe.transpose(bank[3][0:NB, 0:D], rs[:], ident[0:D, 0:D]).then_inc(S["expm_ps"], 1)
                if k == 24:
                    pe.wait_ge(S["expm_pool"], DIAG_DONE)
                    mm(bank[4][0:D, 0:NB * (NSQ + 1)], ones[0:NB, 0:D], dg[:].rearrange("p b t -> p (b t)"),
                       start=True, stop=True).then_inc(S["expm_ps"], 1)
                if k == 26:
                    pe.wait_ge(S["expm_dve"], SCALED_DONE)
                    products(bank[2], Ab, Ab, S["expm_ps"])
                if k == 27:
                    pe.wait_ge(S["expm_act"], A2_DONE)
                    products(bank[3], A2, Ab, S["expm_ps"])
                    pe.wait_ge(S["expm_act"], FLAGS_SPREAD)
                    products(bank[4], A2, A2, S["expm_ps"])
                if k == 28:
                    pe.wait_ge(S["expm_dve"], B2_DONE)
                    pe.wait_ge(S["expm_act"], A4_DONE)
                    products(bank[2], A4, Bk, S["expm_ps"])
                    pe.wait_ge(S["expm_dve"], H1_DONE)
                    products(bank[3], A4, L, S["expm_ps"])
                if k == 30:
                    pe.wait_ge(S["expm_dve"], R_DONE)
                    for b in range(NB):
                        last = pe.transpose(bank[4][0:D, b * D:(b + 1) * D], RR[:, b, :], ident[0:D, 0:D])
                    last.then_inc(S["expm_ps"], 1)
                if SQ0 <= k < SQ0 + 2 * NSQ:
                    t, half = (k - SQ0) // 2, (k - SQ0) % 2
                    if t == 0:
                        pe.wait_ge(S["expm_act"], RT_DONE)
                    else:
                        pe.wait_ge(S["sq_ready"], 2 * t)
                    if half == 0:
                        products(bank[2], RT, RR, S["p_sq"])
                    else:
                        products(bank[3], RR, RT, S["p_sq"])

            def products(dst, lhsT, rhs, done):
                for b in range(NB):
                    last = mm(dst[0:D, b * D:(b + 1) * D], lhsT[:, b, :], rhs[:, b, :], start=True, stop=True)
                last.then_inc(done, 1)

            pe.wait_ge(S["const"], 1)
            pe.wait_ge(S["ld_P"], 16)
            for j in range(D):
                if j:
                    pe.wait_ge(S["upd"], 3 * (j - 1) + 1)
                mm(R[1][0:CH, j:D], bc(ident[0:CH, j:j + 1], [CH, CH]), A[:, 0, j:D], start=True, stop=True)\
                    .then_inc(S["qrE"], 1)
                pe.wait_ge(S["a0"], j + 1)
                mm(R[0][0:CH, j:D], bc(a0m[:, j % 2:j % 2 + 1], [CH, CH]), A[:, 0, j:D], start=True, stop=False)
                for t in (1, 2):
                    if j:
                        pe.wait_ge(S["upd"], 3 * (j - 1) + t + 1)
                    last = mm(R[0][0:CH, j:D], bc(A[:, t, j:j + 1], [CH, CH]), A[:, t, j:D], start=False, stop=(t == 2))
                last.then_inc(S["qrD"], 1)
                side(j)
            pe.wait_ge(S["V_ready"], 1)
            pe.wait_ge(S["sq_ready"], 2 * NSQ)
            for t in range(NCH):
                last = mm(R[0][0:D, 0:D], A[:, t, :], A[:, t, :], start=(t == 0), stop=(t == NCH - 1))
            last.then_inc(S["expm_ps"], 1)
            for t in range(NCH):
                last = pe.transpose(bank[2][0:D, t * CH:(t + 1) * CH], A[:, t, :], ident[0:CH, 0:CH])
            last.then_inc(S["expm_ps"], 1)
            pe.wait_ge(S["expm_dve"], X_DONE)
            pe.transpose(bank[3][0:D, 0:D], XX[:, 0, :], ident[0:D, 0:D]).then_inc(S["expm_ps"], 1)
            for k in range(6):
                pe.wait_ge(S["XT_ready"], k + 1)
                pe.wait_ge(S["Y_ready"], k + 1)
                mm(bank[5][0:D, 0:D], XX[:, 1, :], Y[:], start=True, stop=True).then_inc(S["p_Y"], 1)
                if k < 5:
                    mm(bank[4][0:D, 0:D], XX[:, 1, :], XX[:, 0, :], start=True, stop=True)
                    mm(bank[4][0:D, D:2 * D], XX[:, 0, :], XX[:, 1, :], start=True, stop=True).then_inc(S["p_X"], 1)
            pe.wait_ge(S["Y_ready"], 7)
            for t in range(NCH):
                last = mm(bank[6][0:CH, t * D:(t + 1) * D], VT[:, t * CH:(t + 1) * CH], Y[:], start=True, stop=True)
            last.then_inc(S["p_U"], 1)
            mm(bank[7][0:D, 0:C], Y[:], VT[:], start=True, stop=True).then_inc(S["p_U"], 1)
            pe.wait_ge(S["U_ready"], 4)
            pe.wait_ge(S["rotm"], 1)
            for b in range(NB):
                mm(bank[b][0:D, 0:C], RT[:, b, :], UT[:], start=True, stop=True).then_inc(S["p_rot"], 1)
            pe.wait_ge(S["rot_ready"], NB)

            read = [None, None]

            def ring(k, done, value):
                if read[k % 2] is not None:
                    pe.wait_ge(*read[k % 2])
                read[k % 2] = (done, value)
                return R[k % 2]

            def transposed(i, src, width, ps, readers):
                for c in range(3):
                    rows = min(width, (XW if width == 128 else C) - c * width)
                    r = ring(c, readers, i * 3 + c + 1)
                    for t in range(NT):
                        last = pe.transpose(r[0:rows, t * 128:(t + 1) * 128], src[:, t, c * width:c * width + rows], ident[:])
                    last.then_inc(ps, 1)

            def split_mm(dst, left, right, n):
                (lh, ll), (rh, rl) = left, right
                k = 0
                for c in range(2):
                    for p, q in ((lh, rh), (ll, rh), (lh, rl)):
                        mm(dst, p(c), q(c), start=(k == 0), stop=False)
                        k += 1
                return mm(dst, lh(2), rh(2), start=False, stop=True)

            def f_xT(i):
                pe.wait_ge(S["ld_x"], i * 16 + 16)
                transposed(i, xin, CH, S["xT_ps"], S["xT_sb"])

            def f_z(i):
                pe.wait_ge(S["xT_sb"], i * 3 + 3)
                r = ring(1, S["z_sb"], i + 1)
                for c in range(NCH):
                    last = mm(r[0:D, :], U[:, c, :], xT[:, c, :], start=(c == 0), stop=(c == NCH - 1))
                last.then_inc(S["z_ps"], 1)

            def f_delta(i):
                pe.wait_ge(S["z_sb"], i + 1)
                pe.wait_ge(S["ld_rot"], i * 16 + 16)
                for t in range(NT):
                    r = ring(t, S["xrot"], i * NT + t + 1)
                    mm(r[:, 0:C], zT[:, t * 128:(t + 1) * 128], rot[:], start=True, stop=True).then_inc(S["delta_ps"], 1)

            def f_hT(i):
                pe.wait_ge(S["xh_f1"], i * 8 + 8)
                transposed(i, xh, 128, S["hT_ps"], S["hF"])

            def f_qk(i, tiles=range(MT)):
                pe.wait_ge(S["hHi"], i * 4 + 4)
                pe.wait_ge(S["hLo"], i * 2 + 2)
                for m in tiles:
                    rows = MROWS[m]
                    cols = slice(m * HP * HD, m * HP * HD + rows)
                    r = ring(m + 1, S["qkh"], i * MT + m + 1)
                    split_mm(r[0:rows, :],
                             (lambda c: wqh[0:128 if c < 2 else STACK, c, cols], lambda c: wql[:, c, cols]),
                             (lambda c: Hh[0:128 if c < 2 else STACK, c, :], lambda c: Hl[:, c, :]), 512)\
                        .then_inc(S["qk_ps"], 1)

            def m_v(i):
                for t in range(NT):
                    tok = slice(t * 128, (t + 1) * 128)
                    r = ring(t, S["v_sb"], i * NT + t + 1)
                    split_mm(r[:, 0:C],
                             (lambda c: Hh[0:128 if c < 2 else STACK, c, tok], lambda c: Hl[:, c, tok]),
                             (lambda c: wqh[0:128 if c < 2 else STACK, c, 2 * C:3 * C], lambda c: wql[:, c, 2 * C:3 * C]), C)\
                        .then_inc(S["v_ps"], 1)

            def m_scores(i, h, t):
                r = ring(t, S["smax"], i * 64 + (4 * h + t + 1))
                mm(r[:], Qs[0:KROWS, h, t * 128:(t + 1) * 128], Ks[0:KROWS, h, :], start=True, stop=True)\
                    .then_inc(S["s_ps"], 1)

            def m_shifted(i, h, k):
                if h % 4 == 0 and k == 0:
                    pe.wait_ge(m_in[h // 4 % 2], (i * 2 + (h // 8 + 1)) * 16)
                if h or not fixed(i, 0):
                    pe.wait_ge(S["expd"], i * 32 + (2 * h - 1 + k))
                for n in range(2):
                    kt = 2 * k + n
                    last = mm(ST[k][:, n, :], Ks[0:KROWS + NPART, h, kt * 128:(kt + 1) * 128], Qs[0:KROWS + NPART, h, :],
                              start=True, stop=True)
                last.then_inc(S["st_ps"], 1)

            def m_av(i, h, k):
                if h == 0 and k == 0:
                    pe.wait_ge(S["v_sb"], i * NT + NT)
                if k == 0 and (h or not fixed(i, 0)):
                    pe.wait_ge(S["avT"], i * NH + h)
                pe.wait_ge(S["expd"], i * 32 + (2 * h + k + 1))
                for kt in (2 * k, 2 * k + 1):
                    last = mm(OB[0][0:VW, :], Va[:, kt, h, :], PT[:, h % 2, kt, :], start=(kt == 0), stop=(kt == NT - 1))
                last.then_inc(S["av_ps"], 1)

            def m_tok(i, h):
                p = h // 2
                if h % 2 == 0 and (p or not fixed(i, 0)):
                    pe.wait_ge(S["o_sb"], i * 8 + p)
                wait_apart(pe, S["avT"], i * NH + (h + 1))
                for t in range(NT):
                    last = pe.transpose(tok[:, t, h % 2, :], oTh[:, t * 128:(t + 1) * 128], ident[0:VW, 0:VW])
                last.then_inc(S["tok_ps"], 1)

            def m_mT(i, q):
                pe.wait_ge(S["mparts"], i * 16 + 4 * q + 4)
                r = ring(0, S["mT_sb"], i * 4 + q + 1)
                pe.sem_inc(S["apart"], 1)
                pe.transpose(r[0:48, 0:64].bitcast(BF16), mp[:].rearrange("p k n -> p (k n)"), identb[:])\
                    .then_inc(S["mT_ps"], 1)

            def t_oT(i):
                pe.wait_ge(S["o_sb"], i * 8 + 8)
                transposed(i, o, CH, S["oT_ps"], S["oT_sb"])

            def t_proj(i, tiles=range(NT)):
                pe.wait_ge(S["oT_sb"], i * 3 + 3)
                for t in tiles:
                    r = ring(t, S["yg"], i * 8 + (4 * (t // 2) + t % 2 + 1))
                    for c in range(NCH):
                        last = mm(r[:, 0:C], xT[:, c, t * 128:(t + 1) * 128], wp[:, c, :], start=(c == 0), stop=(c == NCH - 1))
                    last.then_inc(S["proj_ps"], 1)

            def t_nT(i):
                pe.wait_ge(S["xh_n"], i * 8 + 8)
                transposed(i, xh, 128, S["nT_ps"], S["nF"])

            def t_gate(i):
                pe.wait_ge(S["nHi"], i * 4 + 4)
                pe.wait_ge(S["nLo"], i * 2 + 2)
                r = ring(0, S["lgc"], i * 20 + 1)
                for t in range(NT):
                    tok = slice(t * 128, (t + 1) * 128)
                    last = split_mm(r[:, t * NE:(t + 1) * NE],
                                    (lambda c: Nh[0:128 if c < 2 else STACK, c, tok], lambda c: Nl[:, c, tok]),
                                    (lambda c: wgh[0:128 if c < 2 else STACK, c, :], lambda c: wgl[:, c, :]), NE)
                last.then_inc(S["gl_ps"], 1)

            def t_cwT(i):
                pe.wait_ge(S["cw_ready"], i * 6 + 6)
                r = ring(0, S["cwT_sb"], i + 1)
                for t in range(NT):
                    last = pe.transpose(r[0:NE, t * 128:(t + 1) * 128], lg[:, t, :], ident[:])
                last.then_inc(S["cwT_ps"], 1)

            def t_b2(i):
                pe.wait_ge(S["cwT_sb"], i + 1)
                for t in range(NT):
                    r = ring(t + 1, S["b2g"], i * NT + t + 1)
                    mm(r[:, 0:C], zT[0:NE, t * 128:(t + 1) * 128], b2s[:], start=True, stop=True).then_inc(S["b2_ps"], 1)

            def sequence(i, first=False, second=False, last=False):
                for h in range(NH):
                    st, av, tk = (behind(i, h, n, first) for n in (8, 10, 11))
                    if h % 4 == 0:
                        pe.wait_ge(qin[h // 4], (i + 1) * 144)
                    if av:
                        m_av(*av, 0)
                    m_scores(i, h, 0)
                    if st:
                        m_shifted(*st, 0)
                    m_scores(i, h, 1)
                    if tk:
                        m_tok(*tk)
                    if av:
                        m_av(*av, 1)
                    m_scores(i, h, 2)
                    if st:
                        m_shifted(*st, 1)
                    m_scores(i, h, 3)
                    if h % 4 == 0 and (h or not first):
                        m_mT(*quad_before(i, h))
                    if h == XT_AT and not last:
                        f_xT(i + 1)
                    if h == NT_AT and not (first or second):
                        t_nT(i - 2)
                    if h == Z_AT and not last:
                        f_z(i + 1)
                    if h == DELTA_AT and not last:
                        f_delta(i + 1)
                    if h == GATE_AT and not (first or second):
                        t_gate(i - 2)
                    if h == CW_AT and not (first or second):
                        t_cwT(i - 2)
                    if h == HT_AT and not last:
                        f_hT(i + 1)
                    if h == B2_AT and not (first or second):
                        t_b2(i - 2)
                    if h == V_AT:
                        m_v(i)
                    if h == OT_AT and not first:
                        t_oT(i - 1)
                    if h in QK_AT and not last:
                        f_qk(i + 1, QK_AT[h])
                    if h in PROJ_AT and not first:
                        t_proj(i - 1, PROJ_AT[h])

            f_xT(0)
            f_z(0)
            pe.wait_ge(S["wq_split"], 5)
            pe.wait_ge(S["ld_misc"], 16 * (4 + MT))
            f_delta(0)
            f_hT(0)
            f_qk(0)
            pe.wait_ge(S["kones"], 1)
            sequence(0, first=True)
            sequence(1, second=True)
            with pe.Fori(2, NB - 1) as i:
                read[:] = [(S["smax"], i * 64 - 1), (S["smax"], i * 64)]
                sequence(i)
            read[:] = [(S["smax"], (NB - 1) * 64 - 1), (S["smax"], (NB - 1) * 64)]
            sequence(NB - 1, last=True)
            for h in range(8, NH + 3):
                if h - 3 < NH:
                    m_tok(NB - 1, h - 3)
                if h - 2 < NH:
                    m_av(NB - 1, h - 2, 0)
                if h < NH:
                    m_shifted(NB - 1, h, 0)
                if h - 2 < NH:
                    m_av(NB - 1, h - 2, 1)
                if h < NH:
                    m_shifted(NB - 1, h, 1)
                if h == 8:
                    m_mT(NB - 1, 3)
                if h == 8 + NT_AT:
                    t_nT(NB - 2)
                if h == 8 + GATE_AT:
                    t_gate(NB - 2)
                if h == 8 + CW_AT:
                    t_cwT(NB - 2)
                if h == 8 + B2_AT:
                    t_b2(NB - 2)
            t_oT(NB - 1)
            t_proj(NB - 1)
            t_nT(NB - 1)
            t_gate(NB - 1)
            t_cwT(NB - 1)
            t_b2(NB - 1)
            pe.wait_ge(S["x2_2"], NB * NT)

            def group(e, pair, u, later):
                g = e * NB + (pair * 2 + u)
                pe.wait_ge(ld_xn[u], (e * (NB // 2) + pair + 1) * 32)

                def hidden(t):
                    pe.wait_ge(S["w_lo"], e * (3 * HT) + 3 * (t + 1))
                    if later or t >= 3:
                        pe.wait_ge(S["gelu"], g * HT + (t - 2))
                    split_mm(m1_bank(t),
                             (lambda c: w1h[0:128 if c < 2 else STACK, t, c, :], lambda c: w1l[:, t, c, :]),
                             (lambda c: xn[:, u, c, :] if c < 2 else xn[0:STACK, u, 4, :], lambda c: xn[:, u, 2 + c, :]), 512)\
                        .then_inc(S["m1_ps"], 1)

                def combine(t):
                    pe.wait_ge(S["glo"], g * HT + (t + 1))
                    if t == 0 and later:
                        pe.wait_ge(S["eg"], g * NT)
                    for m in range(NT):
                        tok = slice(m * 128, (m + 1) * 128)
                        dst = m2_bank(m)[:, 0:C]
                        mm(dst, Gh[:, t % 3, tok], w2h[:, t, :], start=(t == 0), stop=False)
                        mm(dst, Gh[:, t % 3, tok], w2l[:, t, :], start=False, stop=False)
                        last = mm(dst, Gl[:, t % 3, tok], w2h[:, t, :], start=False, stop=(t == HT - 1))
                    last.then_inc(S["m2_ps"], 1)

                for t in range(HT + 2):
                    if t < HT:
                        hidden(t)
                    if t >= 2:
                        combine(t - 2)

            for u in range(2):
                group(0, 0, u, u > 0)
            with pe.Fori(1, NB // 2) as p:
                for u in range(2):
                    group(0, p, u, True)
            with pe.Fori(1, NE) as e:
                with pe.Fori(0, NB // 2) as p:
                    for u in range(2):
                        group(e, p, u, True)


def kernel(**inputs):
    import numpy as _np
    import concourse.bacc as _bacc
    from concourse.bass_utils import run_bass_kernel_spmd as _run

    get = lambda k: _np.ascontiguousarray(inputs[k])
    W = get("L0_cond_W")
    iu, ju = _np.triu_indices(D, k=1)
    WT = _np.zeros((C, D * D), W.dtype)
    WT[:, iu * D + ju] = W.T
    bU = _np.zeros((D, D), W.dtype)
    bU[iu, ju] = get("L0_cond_b")
    arrays = {
        "x": get("x"), "condT": _np.ascontiguousarray(get("cond_1152").T), "P": get("L0_cond_P"), "WT": WT, "bU": bU,
        "w_adaln": get("L1_cond_w_adaln"), "b_adaln": get("L1_cond_b_adaln"), "w_qkv": get("L1_cond_w_qkv"),
        "b_qkv": get("L1_cond_b_qkv"), "w_proj": get("L1_cond_w_proj"), "b_proj": get("L1_cond_b_proj"),
        "w_gate": get("L1_cond_w_gate"), "w1": get("L1_cond_w1"), "b1T": _np.ascontiguousarray(get("L1_cond_b1").reshape(NE * HT, 128).T), "w2": get("L1_cond_w2"),
        "b2": get("L1_cond_b2"),
    }
    nc = _bacc.Bacc("TRN2", target_bir_lowering=False, num_devices=1)
    args = [nc.dram_tensor(f"in_{k}", a.shape, F32, kind="ExternalInput").ap() for k, a in arrays.items()]
    y = nc.dram_tensor("out_y", (NB, T, C), F32, kind="ExternalOutput").ap()
    build(nc, *args, y)
    r = _run(nc, [{f"in_{k}": a for k, a in arrays.items()}], core_ids=[0])
    return r.results[0]["out_y"]
```
